# Optimizing a Trainium2 kernel written in Bass

```python
import numpy as np
import jax
import jax.numpy as jnp

def _softmax(x, axis=-1):
    return jax.nn.softmax(x, axis=axis)
def _gelu(x):
    return jax.nn.gelu(x, approximate=True)
def _silu(x):
    return jax.nn.silu(x)
def _sigmoid(x):
    return jax.nn.sigmoid(x)
def _layernorm(x, axis=-1, eps=1e-5):
    m = jnp.mean(x, axis=axis, keepdims=True)
    v = jnp.var(x, axis=axis, keepdims=True)
    return (x - m) / jnp.sqrt(v + eps)
def _scatter_add(tgt, idx, src, axis=0):
    return tgt.at[idx].add(src)
def _segment_sum(src, seg, n):
    return jax.ops.segment_sum(src, seg, n)

kernel_name = 'mk_conv_preact_d2_conv_nhwc256_75c35e'

def setup_inputs(seed: int = 0):
    np.random.seed(seed)
    _w = jnp.asarray
    def _rec_inputs():
        import jax
        import jax.numpy as jnp
        _gk = jax.random.key(seed)
        x = -0.0003929 + 0.9999 * jax.random.normal(jax.random.fold_in(_gk, 1), (16, 64, 64, 256), jnp.float32)
        return x
    x = _rec_inputs()
    def _L0_conv_setup():
        import jax, jax.numpy as jnp
        import numpy as np
        B, H, W, C = (16, 64, 64, 256)
        key = jax.random.key(seed)
        ks = jax.random.split(key, 4)
        x = jax.random.normal(ks[0], (B, H, W, C), dtype=jnp.float32)
        w1 = jax.random.normal(ks[1], (C,), dtype=jnp.float32) * C ** (-0.5)
        w2 = jax.random.normal(ks[2], (C,), dtype=jnp.float32) * C ** (-0.5)
        w3 = jax.random.normal(ks[3], (C,), dtype=jnp.float32) * C ** (-0.5)
        b1 = jnp.zeros((1,), jnp.float32)
        b2 = jnp.zeros((1,), jnp.float32)
        b3 = jnp.zeros((1,), jnp.float32)
        return {'x': x, 'w1': w1, 'b1': b1, 'w2': w2, 'b2': b2, 'w3': w3, 'b3': b3}
    _L0_conv_all = _L0_conv_setup()
    _L0_conv_in = {k: v for k, v in _L0_conv_all.items() if k in ('w1', 'b1', 'w2', 'b2', 'w3', 'b3', )}
    del _L0_conv_all

    def _L1_conv_setup():
        import jax, jax.numpy as jnp
        import numpy as np
        D_MODEL = 256
        D_INNER = 512
        D_STATE = 16
        D_CONV = 4
        DT_RANK = 16

        def _mamba_block(x, W_in, conv_w, conv_b, W_xproj, W_dt, b_dt, A_log, D_skip, W_out, ln_w):
            N, T, J, C = x.shape
            res = x
            xr = jnp.transpose(x, (0, 2, 1, 3)).reshape(N * J, T, C)
            B = N * J
            xz = jnp.einsum('btc,ec->bte', xr, W_in)
            xc, z = jnp.split(xz, 2, axis=-1)
            xp = jnp.pad(xc, ((0, 0), (D_CONV - 1, 0), (0, 0)))
            xw = jnp.stack([xp[:, k:k + T, :] for k in range(D_CONV)], axis=-1)
            xc = jnp.einsum('btdk,dk->btd', xw, conv_w) + conv_b
            xc = jax.nn.silu(xc)
            x_dbl = jnp.einsum('btd,ed->bte', xc, W_xproj)
            dt_in = x_dbl[..., :DT_RANK]
            Bm = x_dbl[..., DT_RANK:DT_RANK + D_STATE]
            Cm = x_dbl[..., DT_RANK + D_STATE:]
            dt = jax.nn.softplus(jnp.einsum('btr,dr->btd', dt_in, W_dt) + b_dt)
            A = -jnp.exp(A_log)
            dA = jnp.exp(jnp.einsum('btd,ds->btds', dt, A))
            dBu = jnp.einsum('btd,bts->btds', dt * xc, Bm)

            def step(h, inp):
                dA_t, dBu_t, C_t = inp
                h = dA_t * h + dBu_t
                y = jnp.einsum('bds,bs->bd', h, C_t)
                return (h, y)
            h0 = jnp.zeros((B, D_INNER, D_STATE), xc.dtype)
            _, ys = jax.lax.scan(step, h0, (jnp.swapaxes(dA, 0, 1), jnp.swapaxes(dBu, 0, 1), jnp.swapaxes(Cm, 0, 1)))
            y = jnp.swapaxes(ys, 0, 1)
            y = y + xc * D_skip
            y = y * jax.nn.silu(z)
            out = jnp.einsum('btd,cd->btc', y, W_out)
            out = out * jax.lax.rsqrt(jnp.mean(out * out, axis=-1, keepdims=True) + 1e-06) * ln_w
            out = jnp.transpose(out.reshape(N, J, T, C), (0, 2, 1, 3))
            return out + res
        key = jax.random.key(seed)
        ks = jax.random.split(key, 10)
        N, T, J, C = (8, 64, 25, D_MODEL)
        x = jax.random.normal(ks[0], (N, T, J, C), jnp.float32)
        W_in = jax.random.normal(ks[1], (2 * D_INNER, D_MODEL), jnp.float32) * 0.02
        conv_w = jax.random.normal(ks[2], (D_INNER, D_CONV), jnp.float32) * 0.2
        conv_b = jax.random.normal(ks[3], (D_INNER,), jnp.float32) * 0.02
        W_xproj = jax.random.normal(ks[4], (DT_RANK + 2 * D_STATE, D_INNER), jnp.float32) * 0.02
        W_dt = jax.random.normal(ks[5], (D_INNER, DT_RANK), jnp.float32) * 0.1
        b_dt = jax.random.normal(ks[6], (D_INNER,), jnp.float32) * 0.1 - 4.0
        A_log = jnp.log(jnp.broadcast_to(jnp.arange(1, D_STATE + 1, dtype=jnp.float32), (D_INNER, D_STATE)))
        D_skip = jnp.ones((D_INNER,), jnp.float32)
        W_out = jax.random.normal(ks[7], (D_MODEL, D_INNER), jnp.float32) * 0.02
        ln_w = jnp.ones((D_MODEL,), jnp.float32)
        return {'x': x, 'W_in': W_in, 'conv_w': conv_w, 'conv_b': conv_b, 'W_xproj': W_xproj, 'W_dt': W_dt, 'b_dt': b_dt, 'A_log': A_log, 'D_skip': D_skip, 'W_out': W_out, 'ln_w': ln_w}
    _L1_conv_all = _L1_conv_setup()
    _L1_conv_in = {k: v for k, v in _L1_conv_all.items() if k in ('W_in', 'conv_w', 'conv_b', 'W_xproj', 'W_dt', 'b_dt', 'A_log', 'D_skip', 'W_out', 'ln_w', )}
    del _L1_conv_all

    return {
        "x": x,
        "L0_conv_w1": _L0_conv_in["w1"],
        "L0_conv_b1": _L0_conv_in["b1"],
        "L0_conv_w2": _L0_conv_in["w2"],
        "L0_conv_b2": _L0_conv_in["b2"],
        "L0_conv_w3": _L0_conv_in["w3"],
        "L0_conv_b3": _L0_conv_in["b3"],
        "L1_conv_W_in": _L1_conv_in["W_in"],
        "L1_conv_conv_w": _L1_conv_in["conv_w"],
        "L1_conv_conv_b": _L1_conv_in["conv_b"],
        "L1_conv_W_xproj": _L1_conv_in["W_xproj"],
        "L1_conv_W_dt": _L1_conv_in["W_dt"],
        "L1_conv_b_dt": _L1_conv_in["b_dt"],
        "L1_conv_A_log": _L1_conv_in["A_log"],
        "L1_conv_D_skip": _L1_conv_in["D_skip"],
        "L1_conv_W_out": _L1_conv_in["W_out"],
        "L1_conv_ln_w": _L1_conv_in["ln_w"],
    }

def reference(x, L0_conv_w1, L0_conv_b1, L0_conv_w2, L0_conv_b2, L0_conv_w3, L0_conv_b3, L1_conv_W_in, L1_conv_conv_w, L1_conv_conv_b, L1_conv_W_xproj, L1_conv_W_dt, L1_conv_b_dt, L1_conv_A_log, L1_conv_D_skip, L1_conv_W_out, L1_conv_ln_w):
    import jax
    import jax.numpy as jnp
    def _L0_conv_ref(x, w1, b1, w2, b2, w3, b3):
        import jax, jax.numpy as jnp
        import numpy as np
        B, H, W, C = (16, 64, 64, 256)
        b, h, w, c = x.shape
        n = h * w
        xf = x.reshape(b, n, c)
        x0 = jnp.einsum('bnc,c->bn', xf, w1) + b1[0]
        x1 = jnp.einsum('bnc,c->bn', xf, w2) + b2[0]
        x2 = jnp.einsum('bnc,c->bn', xf, w3) + b3[0]
        sim = x0[:, :, None] * x1[:, None, :]
        sm = jax.nn.softmax(sim, axis=1)
        feats = jnp.einsum('bn,bnm->bm', x2, sm)
        gate = jax.nn.sigmoid(feats).reshape(b, h, w, 1)
        return gate * x

    def _L1_conv_ref(x, W_in, conv_w, conv_b, W_xproj, W_dt, b_dt, A_log, D_skip, W_out, ln_w):
        import jax, jax.numpy as jnp
        import numpy as np
        D_MODEL = 256
        D_INNER = 512
        D_STATE = 16
        D_CONV = 4
        DT_RANK = 16

        def _mamba_block(x, W_in, conv_w, conv_b, W_xproj, W_dt, b_dt, A_log, D_skip, W_out, ln_w):
            N, T, J, C = x.shape
            res = x
            xr = jnp.transpose(x, (0, 2, 1, 3)).reshape(N * J, T, C)
            B = N * J
            xz = jnp.einsum('btc,ec->bte', xr, W_in)
            xc, z = jnp.split(xz, 2, axis=-1)
            xp = jnp.pad(xc, ((0, 0), (D_CONV - 1, 0), (0, 0)))
            xw = jnp.stack([xp[:, k:k + T, :] for k in range(D_CONV)], axis=-1)
            xc = jnp.einsum('btdk,dk->btd', xw, conv_w) + conv_b
            xc = jax.nn.silu(xc)
            x_dbl = jnp.einsum('btd,ed->bte', xc, W_xproj)
            dt_in = x_dbl[..., :DT_RANK]
            Bm = x_dbl[..., DT_RANK:DT_RANK + D_STATE]
            Cm = x_dbl[..., DT_RANK + D_STATE:]
            dt = jax.nn.softplus(jnp.einsum('btr,dr->btd', dt_in, W_dt) + b_dt)
            A = -jnp.exp(A_log)
            dA = jnp.exp(jnp.einsum('btd,ds->btds', dt, A))
            dBu = jnp.einsum('btd,bts->btds', dt * xc, Bm)

            def step(h, inp):
                dA_t, dBu_t, C_t = inp
                h = dA_t * h + dBu_t
                y = jnp.einsum('bds,bs->bd', h, C_t)
                return (h, y)
            h0 = jnp.zeros((B, D_INNER, D_STATE), xc.dtype)
            _, ys = jax.lax.scan(step, h0, (jnp.swapaxes(dA, 0, 1), jnp.swapaxes(dBu, 0, 1), jnp.swapaxes(Cm, 0, 1)))
            y = jnp.swapaxes(ys, 0, 1)
            y = y + xc * D_skip
            y = y * jax.nn.silu(z)
            out = jnp.einsum('btd,cd->btc', y, W_out)
            out = out * jax.lax.rsqrt(jnp.mean(out * out, axis=-1, keepdims=True) + 1e-06) * ln_w
            out = jnp.transpose(out.reshape(N, J, T, C), (0, 2, 1, 3))
            return out + res
        return _mamba_block(x, W_in, conv_w, conv_b, W_xproj, W_dt, b_dt, A_log, D_skip, W_out, ln_w)

    def _gn(v, G=32, eps=1e-5):
        B_, H_, W_, C_ = v.shape
        g = v.reshape(B_, H_, W_, G, C_ // G)
        m = jnp.mean(g, axis=(1, 2, 4), keepdims=True)
        s = jnp.var(g, axis=(1, 2, 4), keepdims=True)
        return ((g - m) / jnp.sqrt(s + eps)).reshape(v.shape)

    def _ln_c(v, eps=1e-6):
        m = jnp.mean(v, axis=-1, keepdims=True)
        s = jnp.var(v, axis=-1, keepdims=True)
        return (v - m) / jnp.sqrt(s + eps)

    def _ln_t(v, eps=1e-5):
        m = jnp.mean(v, axis=-1, keepdims=True)
        s = jnp.var(v, axis=-1, keepdims=True)
        return (v - m) / jnp.sqrt(s + eps)

    def _to_tokens(v):
        B_, H_, W_, C_ = v.shape
        return v.reshape(B_, H_ * W_, C_)
    def _from_tokens(t, like):
        return t.reshape(like.shape)

    x = x + _L0_conv_ref(_gn(x), L0_conv_w1, L0_conv_b1, L0_conv_w2, L0_conv_b2, L0_conv_w3, L0_conv_b3)
    x = x + _L1_conv_ref(_gn(x), L1_conv_W_in, L1_conv_conv_w, L1_conv_conv_b, L1_conv_W_xproj, L1_conv_W_dt, L1_conv_b_dt, L1_conv_A_log, L1_conv_D_skip, L1_conv_W_out, L1_conv_ln_w)
    return x


_drawn_inputs = setup_inputs


def setup_inputs(seed=0):
    import zlib

    import numpy as np

    out = dict(_drawn_inputs(seed))
    spreads = {'L1_conv_D_skip': (1.0, 0.2), 'L1_conv_ln_w': (1.0, 0.2)}
    factors = {'L0_conv_w1': 8.0,
     'L0_conv_w2': 6.685,
     'L0_conv_w3': 4.434,
     'L1_conv_W_xproj': 8.0,
     'L1_conv_W_dt': 8.0,
     'L1_conv_b_dt': 8.0,
     'L1_conv_A_log': 8.0}
    for name, (base, spread) in spreads.items():
        noise = np.random.default_rng([zlib.crc32(name.encode()), seed]).standard_normal(out[name].shape)
        drawn = base * np.exp(spread * noise) if base else spread * noise
        out[name] = jnp.asarray(drawn.astype(out[name].dtype))
    for name, factor in factors.items():
        out[name] = (out[name] * factor).astype(out[name].dtype)
    return out
```

```python
import concourse.bass as bass
from concourse import mybir
from contextlib import ExitStack

F32 = mybir.dt.float32
BF16 = mybir.dt.bfloat16
ALU = mybir.AluOpType
ACT = mybir.ActivationFunctionType
AX = mybir.AxisListType

P = 128
T = 64
J = 64
C = 256
CC = C // P
DI = 512
DK = DI // P
NS = 16
TAPS = 4
R = 16
TOK = T * J
GT = 512
GJ = GT // T
NG = TOK // GT
TILES = TOK // P
GTILES = GT // P
UNITS = NS * DK
BIG_DT = 1.0e25
MIN_A = 1.0e-22

XC_PE = {0: 0, 1: 1, 5: 2, 9: 3}
XC_ACT = {5: 0, 6: 1, 11: 2, 15: 3}
CONV_PE = {4: 0, 8: 1, 12: 2, 13: 3}
CONV_ACT = {10: 0, 14: 1, 18: 2, 19: 3}
Z_PE = {16: 0, 17: 1, 20: 2, 21: 3}
Z_ACT = {21: 0, 22: 1, 25: 2, 26: 3}
SILU_ACT = 27
XD_PE = 28
XD_ACT = 32
DT_PE = {32: 0, 33: 1, 39: 2, 44: 3}
DT_ACT = {36: 0, 41: 1, 46: 2, 51: 3}
DT_DVE = {38: 0, 43: 1, 48: 2, 53: 3}
DT_POOL = {40: 0, 45: 1, 50: 2, 55: 3}
RT_DVE = 45
OUT_PE = {48: 0, 52: 1, 54: 2, 58: 3}
OUT_ACT = {53: 0, 57: 1, 59: 2, 63: 3}
OUT_DVE = {53: 0, 57: 1, 59: 2, 63: 3}

H_CREDIT = 4
PROD_CREDIT = 2
SUM_CREDIT = 4
XT_CREDIT = 4
OUT_CREDIT = 1
STORE_CREDIT = 32
DVE_LINKS = 21


def build(nc, x, w123, b123, win_t, conv_w, conv_b, wxp, wdt_t, b_dt, a_log, d_skip, wout_t, ln_w,
          ident_d, gavg_d, out):
    NB = x.shape[0]
    bc_rows = nc.dram_tensor("bc_rows", (2, 2 * NS, GT), F32, kind="Internal").ap()
    ctx = ExitStack()
    with ctx:
        def sb(name, shape, dt=F32):
            return ctx.enter_context(nc.sbuf_tensor(name, shape, dt))

        def sem(name):
            return ctx.enter_context(nc.semaphore(name))

        ident = sb("ident", [P, P])
        gavg = sb("gavg", [P, P])
        w3 = sb("w3", [P, CC, 3])
        b3 = sb("b3", [P, 3])
        win = sb("win", [P, CC, 2 * DI])
        cw = sb("cw", [P, DK, TAPS])
        cdiag = sb("cdiag", [P, DK, TAPS, P])
        cb = sb("cb", [P, DK])
        wx = sb("wx", [P, DK, P])
        wdt = sb("wdt", [P, DI])
        bdt = sb("bdt", [P, DK])
        alog = sb("alog", [P, DK, NS])
        amat = sb("amat", [P, DK, NS])
        dsk = sb("dsk", [P, DK])
        wout = sb("wout", [P, DK, C])
        lnw = sb("lnw", [P, C])

        xin = sb("xin", [P, 2, GTILES, C])
        xT = sb("xT", [P, CC, TOK])

        arena = sb("arena", [P, 107 * 256])
        place = [0]

        def take(n):
            place[0] += n
            assert place[0] <= arena.shape[1]
            return arena[:, place[0] - n:place[0]]

        dt_sb = take(2 * DI * GT // P).rearrange("p (q k n) -> p q k n", q=2, k=DK)
        u_sb = take(2 * DI * GT // P).rearrange("p (q k n) -> p q k n", q=2, k=DK)
        xc_sb = take(2 * DI * GT // P).rearrange("p (q k n) -> p q k n", q=2, k=DK)
        zs_sb = take(2 * DI * GT // P).rearrange("p (q k n) -> p q k n", q=2, k=DK)
        bc = take(8 * GT).rearrange("p (q i n) -> p q i n", q=4, i=2)
        yg = take(DK * GT).rearrange("p (k n) -> p k n", k=DK)
        g2 = take(CC * GT).rearrange("p (c n) -> p c n", c=CC)
        rt = take(CC * GT).rearrange("p (c n) -> p c n", c=CC)
        te = take(GT)
        tl = take(GT)
        tm = take(GT)
        tc = take(GT)
        xd = take(GT)
        place[0] = 0
        gT = take(CC * TOK).rearrange("p (c n) -> p c n", c=CC)
        x0b = take(TOK)
        x2b = take(TOK)
        ee = take(2 * TOK).rearrange("p (q n) -> p q n", q=2)

        drive = sb("drive", [P, 2, 2, GT])
        prod = sb("prod", [P, 4, GT])
        raw = sb("raw", [P, 2, GJ, TAPS - 1 + T])
        osb = sb("osb", [P, GTILES, C])

        stats = sb("stats", [P, CC, NG, 6])
        mv = sb("mv", [P, CC, 2])
        gs = sb("gs", [P, 2 * CC])
        dev = sb("dev", [P, CC])
        gvar = sb("gvar", [P, CC])
        lnv = sb("lnv", [P, CC])
        y0 = sb("y0", [P, CC])
        nt = sb("nt", [P, 3, CC])
        gn = sb("gn", [P, 2, CC])
        rp1 = sb("rp1", [P, CC])
        x1c = sb("x1c", [P, TILES])
        mxs = sb("mxs", [P, 2, NG])
        mm = sb("mm", [P, 2])
        nm = sb("nm", [P, 3, TILES])
        den = sb("den", [P, TILES])
        num = sb("num", [P, TILES])
        gt4 = sb("gt4", [P, 5, TILES])
        ssq = sb("ssq", [P, GTILES])
        lms = sb("lms", [P, GTILES])
        rms = sb("rms", [P, GTILES])
        sqj = sb("sqj", [P, C])
        eps = sb("eps", [P, 1])
        half_big = sb("half_big", [P, GJ, 1])
        spare = sb("spare", [P, 8])

        psum = ctx.enter_context(nc.psum_tensor("psum", [P, 8, GT], F32))
        ybank = psum[:, 0:DK, :]
        hbank = psum[:, 4:6, :]
        pbank = psum[:, 6:8, :]
        abank = psum[:, 6, :]

        s_w = sem("weights_loaded")
        s_pad = sem("wdt_zeroed")
        s_init = sem("dve_ready")
        s_aexp = sem("a_exponentiated")
        s_wready = sem("weights_ready")
        s_xl = [sem("x_loaded_even"), sem("x_loaded_odd")]
        s_xtf = sem("xt_full")
        s_xtd = sem("xt_done")
        s_mv = sem("moments_ready")
        s_gm = sem("group_means")
        s_dev = sem("deviations")
        s_gd = sem("group_deviations")
        s_var = sem("variances")
        s_ln = sem("act_logs")
        s_y0 = sem("rstd_guess")
        s_gt = sem("gt_ready")
        s_x1f = sem("x1_full")
        s_x1d = sem("x1_done")
        s_x0f = sem("x0_full")
        s_x0d = sem("x0_done")
        s_x2f = sem("x2_full")
        s_x2d = sem("x2_done")
        s_nm = sem("negmax_ready")
        s_e = sem("e_ready")
        s_eu = sem("e_used")
        s_f = sem("feats_ready")
        s_sg = sem("gate_exp")
        s_gate = sem("gate_ready")
        s_gbf = sem("gate_bcast_full")
        s_gx = sem("gate_times_g")
        s_r1 = sem("r1_ready")
        s_g2 = sem("g2_ready")
        s_rt = sem("residual_ready")
        s_xcf = sem("xc_full")
        s_raw = sem("raw_done")
        s_cvf = sem("conv_full")
        s_cvd = sem("conv_done")
        s_zf = sem("z_full")
        s_zd = sem("z_done")
        s_silu = sem("silu_done")
        s_xdf = sem("xd_full")
        s_xdd = sem("xd_done")
        s_rows = sem("bc_rows_stored")
        s_dtf = sem("dt_full")
        s_dtm = sem("dt_evacuated")
        s_de = sem("dt_exp")
        s_dl = sem("dt_log")
        s_corr = sem("dt_corrected")
        s_dt = sem("dt_ready")
        s_u = sem("u_ready")
        s_dtz = sem("dt_first_steps")
        s_bc = [sem(f"bc_loaded{i}") for i in range(4)]
        s_da = sem("decay_ready")
        s_db = sem("drive_ready")
        s_h = sem("h_ready")
        s_pr = sem("prod_ready")
        s_sum = sem("sum_done")
        s_gy = sem("y_gated")
        s_yg = sem("yg_ready")
        s_of = sem("out_full")
        s_sq = sem("square_done")
        s_on = sem("out_normed")
        s_od = sem("out_done")
        s_st = sem("stored")
        s_bn = sem("bn_stats_done")
        s_dch = sem("dve_chain")

        def bc_there(eng, n, s):
            eng.wait_ge(s_bc[s % 4], n * (16 * NS // 4) + (16 * (s // 4) + 16))

        def seq(t4):
            return t4.rearrange("p (j t) -> p j t", t=T)

        block = ctx.enter_context(nc.Block())

        @block.sync
        def _(sp):
            def rows(n, q):
                sp.wait_ge(s_xdd, n + 1)
                sp.dma_start(bc_rows[q], xd[0:2 * NS, :]).then_inc(s_rows, 16)

            def bcast(n, q, s, fresh):
                if s == 0:
                    sp.wait_ge(s_rows, n * 16 + 16)
                if not fresh:
                    sp.wait_ge(s_pr, n * UNITS + (4 * s - 12 + PROD_CREDIT))
                sp.dma_start(bc[:, s % 4, :, :].rearrange("p i n -> p (i n)"),
                             bc_rows[q, 2 * s:2 * s + 2, :].rearrange("(o i) n -> o (i n)", o=1).to_broadcast([P, 2 * GT])
                             ).then_inc(s_bc[s % 4], 16)

            def step(n, q, g, proj):
                for s in range(NS):
                    if s + 2 < NS:
                        bcast(n, q, s + 2, g == 0 and s < 2)
                    elif proj:
                        if s + 2 == NS:
                            rows(n + 1, 1 - q)
                        bcast(n + 1, 1 - q, s + 2 - NS, False)

            def store(ob, n, j0):
                sp.wait_ge(s_od, n * GTILES + (GTILES + OUT_CREDIT))
                for jj in range(2):
                    sp.dma_start(ob[:, strided(j0, jj), :], osb[64 * jj:64 * jj + 64, :, :]).then_inc(s_st, 16)

            def strided(j0, jj):
                if isinstance(j0, int):
                    return slice(j0 + jj, j0 + GJ, 2)
                return bass.ds(j0 + jj, GTILES, 2)

            for dst, src in ((ident[:], ident_d), (gavg[:], gavg_d), 
                             (w3[:], w123.rearrange("(c p) i -> p c i", p=P)),
                             (b3[:], b123.to_broadcast([P, 3])),
                             (win[:], win_t.rearrange("(c p) n -> p c n", p=P)),
                             (cw[:], conv_w.rearrange("(k p) i -> p k i", p=P)),
                             (cb[:], conv_b),
                             (wx[:], wxp.rearrange("(k p) n -> p k n", p=P)),
                             (bdt[:], b_dt),
                             (alog[:], a_log.rearrange("(k p) s -> p k s", p=P)),
                             (dsk[:], d_skip),
                             (wout[:], wout_t.rearrange("(k p) n -> p k n", p=P)),
                             (lnw[:], ln_w.to_broadcast([P, C]))):
                sp.dma_start(dst, src).then_inc(s_w, 16)
            sp.wait_ge(s_pad, 1)
            sp.dma_start(wdt[32:32 + R, :], wdt_t).then_inc(s_w, 16)
            with sp.Fori(0, NB) as b:
                xb = x[bass.ds(b, 1), :, :, :].rearrange("o t j c -> (o t) j c")
                ob = out[bass.ds(b, 1), :, :, :].rearrange("o t j c -> (o t) j c")
                for c in range(NG):
                    sp.wait_ge(s_xtf, b * (NG * CC) + (CC * (c - 2) + CC + XT_CREDIT))
                    for jj in range(2):
                        sp.dma_start(xin[64 * jj:64 * jj + 64, c % 2, :, :],
                                     xb[:, GJ * c + jj:GJ * (c + 1):2, :]).then_inc(s_xl[c % 2], 16)
                n0 = b * NG
                rows(n0, 0)
                bcast(n0, 0, 0, True)
                bcast(n0, 0, 1, True)
                step(n0, 0, 0, True)
                with sp.Fori(0, NG // 2 - 1) as p:
                    n = n0 + 2 * p
                    j0 = 2 * GJ * p
                    step(n + 1, 1, None, True)
                    store(ob, n, j0)
                    step(n + 2, 0, None, True)
                    store(ob, n + 1, j0 + GJ)
                step(n0 + (NG - 1), 1, NG - 1, False)
                store(ob, n0 + (NG - 2), GJ * (NG - 2))
                store(ob, n0 + (NG - 1), GJ * (NG - 1))
            sp.wait_ge(s_st, STORE_CREDIT + NB * NG * 32)

        @block.tensor
        def _(pe):
            def layer0(b):
                for c in range(NG):
                    pe.wait_ge(s_xl[c % 2], b * (NG // 2 * 32) + (c // 2 * 32 + 32))
                    for h in range(CC):
                        q = CC * c + h
                        if q >= 4:
                            pe.wait_ge(s_xtd, b * (NG * CC) + (q - 3))
                        for m in range(GTILES):
                            last = nc.tensor.transpose(psum[:, q % 4, m * P:(m + 1) * P],
                                                       xin[:, c % 2, m, h * P:(h + 1) * P], ident[:])
                            if m == GTILES - 1:
                                last.then_inc(s_xtf, 1)
                group_stats(b, 0)
                for c in range(NG):
                    for h in range(CC):
                        pe.wait_ge(s_gt, b * (NG * CC) + (CC * c + h + 1))
                    if c == 0:
                        pe.wait_ge(s_xtd, (b + 1) * (NG * CC))
                    if c >= 2:
                        pe.wait_ge(s_x1d, b * NG + (c - 1))
                    for m in range(GTILES):
                        for h in range(CC):
                            last = nc.tensor.matmul(psum[:, 6 + c % 2, m * P:(m + 1) * P],
                                                    gT[:, h, (GTILES * c + m) * P:(GTILES * c + m + 1) * P],
                                                    w3[:, h, 1:2].to_broadcast([P, P]),
                                                    start=(h == 0), stop=(h == CC - 1))
                    last.then_inc(s_x1f, 1)
                    for which, full, done in ((0, s_x0f, s_x0d), (2, s_x2f, s_x2d)):
                        if c >= 2:
                            pe.wait_ge(done, b * NG + (c - 1))
                        for h in range(CC):
                            last = nc.tensor.matmul(psum[:, which + c % 2, :],
                                                    w3[:, h, which:which + 1].to_broadcast([P, P]),
                                                    gT[:, h, c * GT:(c + 1) * GT],
                                                    start=(h == 0), stop=(h == CC - 1))
                        last.then_inc(full, 1)
                pe.wait_ge(s_gate, b + 1)
                for c in range(NG):
                    if c >= 4:
                        pe.wait_ge(s_gx, b * (NG * CC) + CC * (c - 3))
                    for m in range(GTILES):
                        i = GTILES * c + m
                        last = nc.tensor.matmul(psum[:, c % 4, m * P:(m + 1) * P],
                                                gt4[:, 4, i:i + 1].to_broadcast([P, P]), ident[:],
                                                start=True, stop=True)
                    last.then_inc(s_gbf, 1)
                group_stats(b, 1)

            def group_stats(b, layer):
                pe.wait_ge(s_mv, 2 * b + (layer + 1))
                nc.tensor.matmul(abank[:, 0:4], gavg[:], mv[:, :, :].rearrange("p c i -> p (c i)"),
                                 start=True, stop=True).then_inc(s_gm, 1)
                pe.wait_ge(s_dev, 2 * b + (layer + 1))
                nc.tensor.matmul(abank[:, 8:10], gavg[:], dev[:], start=True, stop=True).then_inc(s_gd, 1)

            def project(v, n, q, g):
                if v in XC_PE:
                    i = XC_PE[v]
                    if i == 0:
                        pe.wait_ge(s_g2, n + 1)
                        if g != 0:
                            pe.wait_ge(s_dtm, n * DK)
                        if g not in (0, 1, 2):
                            pe.wait_ge(s_od, (n - 2) * GTILES + OUT_CREDIT)
                    if i >= 2:
                        pe.wait_ge(s_raw, n * DK + i)
                    for h in range(CC):
                        last = nc.tensor.matmul(pbank[:, min(i, 1), :], win[:, h, i * P:(i + 1) * P], g2[:, h, :],
                                                start=(h == 0), stop=(h == CC - 1))
                    last.then_inc(s_xcf, 1)
                if v in CONV_PE:
                    i = CONV_PE[v]
                    pe.wait_ge(s_raw, n * DK + (i + 1))
                    if i in (1, 2):
                        pe.wait_ge(s_cvd, n * DK + i)
                    for tap in range(TAPS):
                        last = nc.tensor.matmul(seq(pbank[:, i // 3, :]), cdiag[:, i, tap, :],
                                                raw[:, i % 2, :, tap:tap + T], start=(tap == 0),
                                                stop=(tap == TAPS - 1))
                    last.then_inc(s_cvf, 1)
                if v in Z_PE:
                    i = Z_PE[v]
                    if i < 2:
                        pe.wait_ge(s_cvd, n * DK + (3 + i))
                    else:
                        pe.wait_ge(s_zd, n * DK + (i - 1))
                    for h in range(CC):
                        last = nc.tensor.matmul(pbank[:, i % 2, :], win[:, h, DI + i * P:DI + (i + 1) * P],
                                                g2[:, h, :], start=(h == 0), stop=(h == CC - 1))
                    last.then_inc(s_zf, 1)
                if v == XD_PE:
                    pe.wait_ge(s_zd, n * DK + 3)
                    pe.wait_ge(s_silu, n * 2 + 1)
                    for k in range(DK):
                        last = nc.tensor.matmul(pbank[:, 0, :], wx[:, k, :], xc_sb[:, q, k, :],
                                                start=(k == 0), stop=(k == DK - 1))
                    last.then_inc(s_xdf, 1)
                if v in DT_PE:
                    i = DT_PE[v]
                    if i < 2:
                        pe.wait_ge(s_xdd, n + 1)
                        pe.wait_ge(s_zd, n * DK + DK)
                    else:
                        pe.wait_ge(s_dtm, n * DK + (i - 1))
                    nc.tensor.matmul(pbank[:, 1 - i % 2, :], wdt[:, i * P:(i + 1) * P], xd, start=True,
                                     stop=True).then_inc(s_dtf, 1)

            def output(v, n, proj):
                if v in OUT_PE:
                    i = OUT_PE[v]
                    if i == 0:
                        pe.wait_ge(s_yg, n * DK + DK)
                        pe.wait_ge(s_rt, n + 1)
                    if i < 2 and proj:
                        pe.wait_ge(s_dtm, (n + 2) * DK + (3 + i))
                    elif i < 2:
                        pe.wait_ge(s_od, n * GTILES + OUT_CREDIT)
                    else:
                        pe.wait_ge(s_od, n * GTILES + (i - 1 + OUT_CREDIT))
                    bank = pbank[:, 1 - i % 2, :]
                    for k in range(DK):
                        nc.tensor.matmul(bank[:, 0:C], yg[:, k, i * P:(i + 1) * P], wout[:, k, :],
                                         start=(k == 0), stop=(k == DK - 1))
                    for h in range(CC):
                        last = nc.tensor.transpose(bank[:, C + h * P:C + (h + 1) * P],
                                                   rt[:, h, i * P:(i + 1) * P], ident[:])
                    last.then_inc(s_of, 1)

            def step(n, q, g, proj, outp):
                for v in range(UNITS):
                    s, k = divmod(v, DK)
                    pe.wait_ge(s_pr, n * UNITS + (v + 1 + PROD_CREDIT))
                    if s == 0 and g != 0:
                        pe.wait_ge(s_gy, n * DK + (k + 1 - DK))
                    nc.tensor.matmul(ybank[:, k, :], ident[:], prod[:, v % 4, :], start=(s == 0),
                                     stop=(s == NS - 1)).then_inc(s_sum, 1)
                    if proj:
                        project(v, n + 1, 1 - q, -1 if g is None else g + 1)
                    if outp:
                        output(v, n - 1, proj)

            pe.wait_ge(s_w, 16 * 14)
            pe.wait_ge(s_wready, 1)
            with pe.Fori(0, NB) as b:
                n0 = b * NG
                layer0(b)
                for v in range(UNITS):
                    project(v, n0, 0, 0)
                step(n0, 0, 0, True, False)
                with pe.Fori(0, NG // 2 - 1) as p:
                    n = n0 + 2 * p
                    step(n + 1, 1, None, True, True)
                    step(n + 2, 0, None, True, True)
                step(n0 + (NG - 1), 1, NG - 1, False, True)
                for v in range(UNITS):
                    output(v, n0 + (NG - 1), False)
                pe.wait_ge(s_od, (b + 1) * (NG * GTILES) + OUT_CREDIT)

        @block.scalar
        def _(act):
            def exp_ln_table():
                nc.scalar.preload_act_table_set("natural_log_exp_and_others")

            def group_stats(b, layer):
                act.wait_ge(s_var, 2 * b + (layer + 1))
                nc.scalar.activation(lnv[:], gvar[:], ACT.Ln).then_inc(s_ln, 1)
                act.wait_ge(s_ln, 2 * b + (layer + 1))
                nc.scalar.activation(y0[:], lnv[:], ACT.Exp, scale=-0.5).then_inc(s_y0, 1)

            def layer0(b):
                for c in range(NG):
                    for h in range(CC):
                        q = CC * c + h
                        act.wait_ge(s_xtf, b * (NG * CC) + (q + 1 + XT_CREDIT))
                        nc.scalar.activation(xT[:, h, c * GT:(c + 1) * GT], psum[:, q % 4, :],
                                             ACT.Copy).then_inc(s_xtd, 1)
                group_stats(b, 0)
                for c in range(NG):
                    act.wait_ge(s_x0f, b * NG + (c + 1))
                    nc.scalar.activation(x0b[:, c * GT:(c + 1) * GT], psum[:, c % 2, :], ACT.Identity,
                                         bias=b3[:, 0:1]).then_inc(s_x0d, 1)
                act.wait_ge(s_nm, b + 1)
                act.wait_ge(s_x0d, b * NG + NG)
                for i in range(TILES):
                    if i >= 2:
                        act.wait_ge(s_eu, b * TILES + (i - 1))
                    nc.scalar.activation(ee[:, i % 2, :], x0b, ACT.Exp, bias=nm[:, 2, i:i + 1],
                                         scale=x1c[:, i:i + 1], accum_out=den[:, i:i + 1]).then_inc(s_e, 1)
                act.wait_ge(s_f, b + 1)
                nc.scalar.activation(gt4[:, 2, :], gt4[:, 1, :], ACT.Exp, scale=-1.0).then_inc(s_sg, 1)
                group_stats(b, 1)

            def project(v, n, q, first):
                if v in CONV_ACT:
                    i = CONV_ACT[v]
                    act.wait_ge(s_cvf, n * DK + (i + 1))
                    if i == 0 and not first:
                        act.wait_ge(s_yg, (n - 1) * DK)
                    nc.scalar.activation(xc_sb[:, q, i, :], pbank[:, i // 3, :], ACT.Identity,
                                         bias=cb[:, i:i + 1]).then_inc(s_cvd, 1)
                if v in XC_ACT:
                    i = XC_ACT[v]
                    act.wait_ge(s_xcf, n * DK + (i + 1))
                    if i >= 2:
                        act.wait_ge(s_cvf, n * DK + (i - 1))
                    nc.scalar.activation(raw[:, i % 2, :, TAPS - 1:], seq(pbank[:, min(i, 1), :]),
                                         ACT.Copy).then_inc(s_raw, 1)
                if v in Z_ACT:
                    i = Z_ACT[v]
                    act.wait_ge(s_zf, n * DK + (i + 1))
                    nc.scalar.activation(zs_sb[:, q, i, :], pbank[:, i % 2, :], ACT.Copy).then_inc(s_zd, 1)
                if v == SILU_ACT:
                    act.wait_ge(s_cvd, n * DK + DK)
                    nc.scalar.activation(xc_sb[:, q, :, :], xc_sb[:, q, :, :], ACT.Silu).then_inc(s_silu, 1)
                    act.wait_ge(s_zd, n * DK + DK)
                    nc.scalar.activation(zs_sb[:, q, :, :], zs_sb[:, q, :, :], ACT.Silu).then_inc(s_silu, 1)
                    exp_ln_table()
                if v == XD_ACT:
                    act.wait_ge(s_xdf, n + 1)
                    nc.scalar.activation(xd, pbank[:, 0, :], ACT.Copy).then_inc(s_xdd, 1)
                if v in DT_ACT:
                    i = DT_ACT[v]
                    act.wait_ge(s_dtf, n * DK + (i + 1))
                    if not (first and i == 0):
                        act.wait_ge(s_dt, n * DK + i)
                    nc.scalar.activation(te, pbank[:, 1 - i % 2, :], ACT.Abs, bias=bdt[:, i:i + 1])
                    nc.scalar.activation(tm, pbank[:, 1 - i % 2, :], ACT.Relu, bias=bdt[:, i:i + 1]).then_inc(s_dtm, 1)
                if v - 1 in DT_ACT:
                    i = DT_ACT[v - 1]
                    act.wait_ge(s_dtm, n * DK + (i + 1))
                    nc.scalar.activation(te, te, ACT.Exp, scale=-1.0).then_inc(s_de, 1)
                if v - 2 in DT_ACT:
                    i = DT_ACT[v - 2]
                    act.wait_ge(s_de, n * DK + (i + 1))
                    nc.scalar.activation(tl, te, ACT.Ln, bias=1.0).then_inc(s_dl, 1)

            def output(v, n):
                if v in OUT_ACT:
                    i = OUT_ACT[v]
                    act.wait_ge(s_of, n * GTILES + (i + 1))
                    nc.scalar.activation(sqj[:], pbank[:, 1 - i % 2, 0:C], ACT.Square,
                                         accum_out=ssq[:, i:i + 1]).then_inc(s_sq, 1)
                    act.wait_ge(s_sq, n * (3 * GTILES) + (3 * i + 1))
                    nc.scalar.activation(lms[:, i:i + 1], ssq[:, i:i + 1], ACT.Ln, scale=1.0 / C,
                                         bias=eps[:, 0:1]).then_inc(s_sq, 1)
                    act.wait_ge(s_sq, n * (3 * GTILES) + (3 * i + 2))
                    nc.scalar.activation(rms[:, i:i + 1], lms[:, i:i + 1], ACT.Exp, scale=-0.5).then_inc(s_sq, 1)

            def step(n, q, g, proj, outp):
                for v in range(UNITS):
                    s, k = divmod(v, DK)
                    if s == 0:
                        act.wait_ge(s_dtz, n * DK + (k + 1))
                    act.wait_ge(s_pr, n * UNITS + (v - 1 + PROD_CREDIT))
                    nc.scalar.activation(hbank[:, v % 2, :], dt_sb[:, q, k, :], ACT.Exp,
                                         scale=amat[:, k, s:s + 1]).then_inc(s_da, 1)
                    if proj:
                        project(v, n + 1, 1 - q, g == 0)
                    if outp:
                        output(v, n - 1)

            act.wait_ge(s_w, 16 * 14)
            nc.scalar.activation(amat[:], alog[:], ACT.Exp).then_inc(s_aexp, 1)
            act.wait_ge(s_wready, 1)
            with act.Fori(0, NB) as b:
                n0 = b * NG
                exp_ln_table()
                layer0(b)
                for v in range(UNITS):
                    project(v, n0, 0, True)
                step(n0, 0, 0, True, False)
                with act.Fori(0, NG // 2 - 1) as p:
                    n = n0 + 2 * p
                    exp_ln_table()
                    step(n + 1, 1, None, True, True)
                    step(n + 2, 0, None, True, True)
                exp_ln_table()
                step(n0 + (NG - 1), 1, NG - 1, False, True)
                for v in range(UNITS):
                    output(v, n0 + (NG - 1))
                act.wait_ge(s_of, (b + 1) * (NG * GTILES))

        @block.gpsimd
        def _(pool):
            def project(v, n, q):
                if v in DT_POOL:
                    i = DT_POOL[v]
                    pool.wait_ge(s_corr, n * (3 * DK) + (3 * i + 3))
                    nc.gpsimd.tensor_tensor(dt_sb[:, q, i, :], tc, tm, ALU.add).then_inc(s_dt, 1)
                    pool.wait_ge(s_dt, n * DK + (i + 1))
                    nc.gpsimd.tensor_tensor(u_sb[:, q, i, :], dt_sb[:, q, i, :], xc_sb[:, q, i, :],
                                            ALU.mult).then_inc(s_u, 1)
                    pool.wait_ge(s_u, n * DK + (i + 1))
                    nc.gpsimd.tensor_tensor(seq(dt_sb[:, q, i, :])[:, :, 0:1], half_big[:], half_big[:],
                                            ALU.add).then_inc(s_dtz, 1)

            def gate(n, q, k):
                pool.wait_ge(s_gy, n * DK + (k + 1))
                nc.gpsimd.tensor_tensor(yg[:, k, :], yg[:, k, :], zs_sb[:, q, k, :], ALU.mult).then_inc(s_yg, 1)

            def step(n, q, proj, gate_prev):
                for v in range(0, UNITS, 2):
                    s, k = divmod(v, DK)
                    if s == 0:
                        pool.wait_ge(s_u, n * DK + (k + 2))
                    bc_there(pool, n, s)
                    pool.wait_ge(s_h, n * UNITS + (v - 2 + H_CREDIT))
                    nc.gpsimd.tensor_tensor(drive[:, (v // 2) % 2, :, :], u_sb[:, q, k:k + 2, :],
                                            bc[:, s % 4, 0:1, :].to_broadcast([P, 2, GT]),
                                            ALU.mult).then_inc(s_db, 1)
                    if gate_prev and v in (2, 4):
                        for kg in (v - 2, v - 1):
                            gate(n - 1, 1 - q, kg)
                    if proj:
                        for w in (v, v + 1):
                            project(w, n + 1, 1 - q)

            with pool.Fori(0, NB) as b:
                n0 = b * NG
                for c in range(NG):
                    for h in range(CC):
                        pool.wait_ge(s_gx, b * (NG * CC) + (CC * c + h + 1))
                        nc.gpsimd.tensor_tensor(xT[:, h, c * GT:(c + 1) * GT], xT[:, h, c * GT:(c + 1) * GT],
                                                gT[:, h, c * GT:(c + 1) * GT], ALU.add).then_inc(s_r1, 1)
                for v in range(UNITS):
                    project(v, n0, 0)
                step(n0, 0, True, False)
                with pool.Fori(0, NG // 2 - 1) as p:
                    n = n0 + 2 * p
                    step(n + 1, 1, True, True)
                    step(n + 2, 0, True, True)
                step(n0 + (NG - 1), 1, False, True)
                for k in range(DK):
                    gate(n0 + (NG - 1), 1, k)

        @block.vector
        def _(dve):
            def group_stats(b, layer):
                dve.wait_ge(s_bn, b * (2 * NG * CC) + (layer + 1) * NG * CC)
                nc.vector.tensor_copy(spare[:, 7:8], stats[:, 0, 0, 0:1])
                for h in range(CC):
                    last = nc.vector.bn_aggr(mv[:, h, :], stats[:, h, :, :].rearrange("p c i -> p (c i)"))
                last.then_inc(s_mv, 1)
                dve.wait_ge(s_gm, 2 * b + (layer + 1))
                link(b, nc.vector.tensor_copy(gs[:], abank[:, 0:4]))
                gsv = gs[:].rearrange("p (c i) -> p c i", c=CC)
                link(b, nc.vector.tensor_tensor(nt[:, 0, :], mv[:, :, 0], gsv[:, :, 0], ALU.subtract))
                nc.vector.tensor_tensor(dev[:], nt[:, 0, :], nt[:, 0, :], ALU.mult).then_inc(s_dev, 1)
                dve.wait_ge(s_gd, 2 * b + (layer + 1))
                nc.vector.scalar_tensor_tensor(out=gvar[:], in0=abank[:, 8:10], scalar=1e-5, in1=gsv[:, :, 1],
                                               op0=ALU.add, op1=ALU.add).then_inc(s_var, 1)
                dve.wait_ge(s_y0, 2 * b + (layer + 1))
                link(b, nc.vector.tensor_tensor(nt[:, 0, :], y0[:], y0[:], ALU.mult))
                link(b, nc.vector.tensor_tensor(nt[:, 1, :], nt[:, 0, :], gvar[:], ALU.mult))
                link(b, nc.vector.tensor_scalar(nt[:, 0, :], nt[:, 1, :], -0.5, 1.5, ALU.mult, ALU.add))
                link(b, nc.vector.tensor_tensor(gn[:, 0, :], y0[:], nt[:, 0, :], ALU.mult))
                link(b, nc.vector.scalar_tensor_tensor(out=gn[:, 1, :], in0=gsv[:, :, 0], scalar=-1.0,
                                                       in1=gn[:, 0, :], op0=ALU.mult, op1=ALU.mult))

            count = [0]

            def link(b, ins):
                count[0] += 1
                ins.then_inc(s_dch, 1)
                dve.wait_ge(s_dch, b * DVE_LINKS + count[0])

            def layer0(b):
                for c in range(NG):
                    for h in range(CC):
                        dve.wait_ge(s_xtd, b * (NG * CC) + (CC * c + h + 1))
                        nc.vector.bn_stats(stats[:, h, c, :], xT[:, h, c * GT:(c + 1) * GT]).then_inc(s_bn, 1)
                group_stats(b, 0)
                for c in range(NG):
                    for h in range(CC):
                        nc.vector.tensor_scalar(gT[:, h, c * GT:(c + 1) * GT], xT[:, h, c * GT:(c + 1) * GT],
                                                gn[:, 0, h:h + 1], gn[:, 1, h:h + 1], ALU.mult,
                                                ALU.add).then_inc(s_gt, 1)
                for c in range(NG):
                    dve.wait_ge(s_x1f, b * NG + (c + 1))
                    nc.vector.tensor_scalar(x1c[:, GTILES * c:GTILES * (c + 1)],
                                            psum[:, 6 + c % 2, :].rearrange("p (m n) -> p m n", n=P)[:, :, 0],
                                            b3[:, 1:2], None, ALU.add).then_inc(s_x1d, 1)
                    dve.wait_ge(s_x2f, b * NG + (c + 1))
                    nc.vector.tensor_scalar(x2b[:, c * GT:(c + 1) * GT], psum[:, 2 + c % 2, :],
                                            b3[:, 2:3], None, ALU.add).then_inc(s_x2d, 1)
                    dve.wait_ge(s_x0d, b * NG + (c + 1))
                    nc.vector.tensor_reduce(mxs[:, 0, c:c + 1], x0b[:, c * GT:(c + 1) * GT], AX.X, ALU.max)
                    last = nc.vector.tensor_reduce(mxs[:, 1, c:c + 1], x0b[:, c * GT:(c + 1) * GT], AX.X, ALU.min)
                link(b, last)
                nc.vector.tensor_reduce(mm[:, 0:1], mxs[:, 0, :], AX.X, ALU.max)
                link(b, nc.vector.tensor_reduce(mm[:, 1:2], mxs[:, 1, :], AX.X, ALU.min))
                nc.vector.tensor_scalar(nm[:, 0, :], x1c[:], mm[:, 0:1], None, ALU.mult)
                link(b, nc.vector.tensor_scalar(nm[:, 1, :], x1c[:], mm[:, 1:2], None, ALU.mult))
                link(b, nc.vector.tensor_tensor(nm[:, 0, :], nm[:, 0, :], nm[:, 1, :], ALU.max))
                nc.vector.tensor_scalar(nm[:, 2, :], nm[:, 0, :], -1.0, None, ALU.mult).then_inc(s_nm, 1)
                for i in range(TILES):
                    dve.wait_ge(s_e, b * TILES + (i + 1))
                    nc.vector.tensor_tensor_reduce(out=ee[:, i % 2, :], in0=ee[:, i % 2, :], in1=x2b, scale=1.0,
                                                   scalar=0.0, op0=ALU.mult, op1=ALU.add,
                                                   accum_out=num[:, i:i + 1]).then_inc(s_eu, 1)
                dve.wait_ge(s_eu, b * TILES + TILES)
                link(b, nc.vector.reciprocal(gt4[:, 0, :], den[:]))
                nc.vector.tensor_tensor(gt4[:, 1, :], num[:], gt4[:, 0, :], ALU.mult).then_inc(s_f, 1)
                dve.wait_ge(s_sg, b + 1)
                link(b, nc.vector.tensor_scalar(gt4[:, 3, :], gt4[:, 2, :], 1.0, None, ALU.add))
                nc.vector.reciprocal(gt4[:, 4, :], gt4[:, 3, :]).then_inc(s_gate, 1)
                for c in range(NG):
                    dve.wait_ge(s_gbf, b * NG + (c + 1))
                    for h in range(CC):
                        nc.vector.tensor_tensor(gT[:, h, c * GT:(c + 1) * GT], gT[:, h, c * GT:(c + 1) * GT],
                                                psum[:, c % 4, :], ALU.mult).then_inc(s_gx, 1)
                    if c:
                        r1_stats(b, c - 1)
                r1_stats(b, NG - 1)
                group_stats(b, 1)
                link(b, nc.vector.tensor_scalar(rp1[:], gn[:, 0, :], 1.0, None, ALU.add))

            def r1_stats(b, c):
                for h in range(CC):
                    dve.wait_ge(s_r1, b * (NG * CC) + (CC * c + h + 1))
                    nc.vector.bn_stats(stats[:, h, c, :], xT[:, h, c * GT:(c + 1) * GT]).then_inc(s_bn, 1)

            def span(g):
                return slice(g * GT, (g + 1) * GT) if isinstance(g, int) else bass.ds(g * GT, GT)

            def normalise(n, g_in_batch, first):
                if not first:
                    dve.wait_ge(s_zf, n * DK)
                for h in range(CC):
                    last = nc.vector.tensor_scalar(g2[:, h, :], xT[:, h, span(g_in_batch)],
                                                   gn[:, 0, h:h + 1], gn[:, 1, h:h + 1], ALU.mult, ALU.add)
                last.then_inc(s_g2, 1)

            def residual(n, g_in_batch):
                for h in range(CC):
                    last = nc.vector.tensor_scalar(rt[:, h, :], xT[:, h, span(g_in_batch)],
                                                   rp1[:, h:h + 1], gn[:, 1, h:h + 1], ALU.mult, ALU.add)
                last.then_inc(s_rt, 1)

            def project(v, n):
                if v in DT_DVE:
                    i = DT_DVE[v]
                    dve.wait_ge(s_dl, n * DK + (i + 1))
                    nc.vector.tensor_scalar(tc, te, 1.0, 1.0, ALU.add, ALU.subtract).then_inc(s_corr, 1)
                    dve.wait_ge(s_corr, n * (3 * DK) + (3 * i + 1))
                    nc.vector.tensor_tensor(tc, te, tc, ALU.subtract).then_inc(s_corr, 1)
                    dve.wait_ge(s_corr, n * (3 * DK) + (3 * i + 2))
                    nc.vector.tensor_tensor(tc, tl, tc, ALU.add).then_inc(s_corr, 1)

            def output(v, n):
                if v in OUT_DVE:
                    i = OUT_DVE[v]
                    bank = pbank[:, 1 - i % 2, :]
                    dve.wait_ge(s_sq, n * (3 * GTILES) + (3 * i + 3))
                    if i == 0:
                        dve.wait_ge(s_st, n * 32 + STORE_CREDIT)
                    nc.vector.scalar_tensor_tensor(out=osb[:, i, :], in0=bank[:, 0:C], scalar=rms[:, i:i + 1],
                                                   in1=lnw[:], op0=ALU.mult, op1=ALU.mult).then_inc(s_on, 1)
                    dve.wait_ge(s_on, n * GTILES + (i + 1))
                    nc.vector.tensor_tensor(osb[:, i, :], osb[:, i, :], bank[:, C:2 * C],
                                            ALU.add).then_inc(s_od, 1)

            def gate(n, q, k):
                dve.wait_ge(s_sum, n * UNITS + (UNITS - DK + k + 1 + SUM_CREDIT))
                nc.vector.scalar_tensor_tensor(out=yg[:, k, :], in0=xc_sb[:, q, k, :], scalar=dsk[:, k:k + 1],
                                               in1=ybank[:, k, :], op0=ALU.mult, op1=ALU.add).then_inc(s_gy, 1)

            def step(n, q, g_in_batch, proj, prev):
                if proj:
                    normalise(n + 1, g_in_batch + 1, False)
                for v in range(UNITS):
                    s, k = divmod(v, DK)
                    dve.wait_ge(s_da, n * UNITS + (v + 1))
                    if v % 2 == 0:
                        dve.wait_ge(s_db, n * (UNITS // 2) + (v // 2 + 1))
                    nc.vector.tensor_tensor_scan(hbank[:, v % 2, :], hbank[:, v % 2, :],
                                                 drive[:, (v // 2) % 2, v % 2, :], 0.0, ALU.mult,
                                                 ALU.add).then_inc(s_h, 1)
                    if k == 0:
                        bc_there(dve, n, s)
                    dve.wait_ge(s_sum, n * UNITS + (v - 3 + SUM_CREDIT))
                    dve.wait_ge(s_h, n * UNITS + (v + 1 + H_CREDIT))
                    nc.vector.tensor_tensor(prod[:, v % 4, :], hbank[:, v % 2, :], bc[:, s % 4, 1, :],
                                            ALU.mult).then_inc(s_pr, 1)
                    if prev and v < DK:
                        gate(n - 1, 1 - q, v)
                    if proj:
                        project(v, n + 1)
                    if prev:
                        if v == RT_DVE:
                            residual(n - 1, g_in_batch - 1)
                        output(v, n - 1)

            nc.vector.memset(wdt[:], 0.0).then_inc(s_pad, 1)
            nc.vector.memset(eps[:], 1e-6)
            nc.vector.memset(half_big[:], BIG_DT / 2)
            nc.vector.memset(raw[:], 0.0)
            for i, (credited, credit) in enumerate(((s_h, H_CREDIT), (s_pr, PROD_CREDIT), (s_sum, SUM_CREDIT),
                                                    (s_xtf, XT_CREDIT), (s_od, OUT_CREDIT),
                                                    (s_st, STORE_CREDIT))):
                nc.vector.memset(spare[:, i:i + 1], 0.0).then_inc(credited, credit)
            dve.wait_ge(s_w, 16 * 14)
            for k in range(DK):
                for tap in range(TAPS):
                    nc.vector.tensor_scalar(cdiag[:, k, tap, :], ident[:], cw[:, k, tap:tap + 1], None, ALU.mult)
            dve.wait_ge(s_aexp, 1)
            nc.vector.tensor_scalar(amat[:], amat[:], MIN_A, -1.0, ALU.max, ALU.mult).then_inc(s_wready, 1)
            dve.wait_ge(s_wready, 1)
            with dve.Fori(0, NB) as b:
                n0 = b * NG
                layer0(b)
                normalise(n0, 0, True)
                for v in range(UNITS):
                    project(v, n0)
                step(n0, 0, 0, True, False)
                with dve.Fori(0, NG // 2 - 1) as p:
                    n = n0 + 2 * p
                    step(n + 1, 1, 2 * p + 1, True, True)
                    step(n + 2, 0, 2 * p + 2, True, True)
                step(n0 + (NG - 1), 1, NG - 1, False, True)
                for k in range(DK):
                    gate(n0 + (NG - 1), 1, k)
                residual(n0 + (NG - 1), NG - 1)
                for v in range(UNITS):
                    output(v, n0 + (NG - 1))
                assert count[0] == DVE_LINKS, count


def _arrays(i):
    import numpy as np
    f = lambda a: np.ascontiguousarray(np.asarray(a))
    cols = lambda a: f(np.asarray(a).reshape(DK, P).T)
    wxp = f(i["L1_conv_W_xproj"])
    dt_rows, bc_rows = wxp[:R], wxp[R:]
    lay = np.zeros((DI, P), np.float32)
    lay[:, 0:2 * NS:2] = bc_rows[:NS].T
    lay[:, 1:2 * NS:2] = bc_rows[NS:].T
    lay[:, 2 * NS:2 * NS + R] = dt_rows.T
    return {
        "x": f(i["x"]),
        "w123": f(np.stack([i["L0_conv_w1"], i["L0_conv_w2"], i["L0_conv_w3"]], 1)),
        "b123": f(np.concatenate([i["L0_conv_b1"], i["L0_conv_b2"], i["L0_conv_b3"]])[None, :]),
        "win_t": f(np.asarray(i["L1_conv_W_in"]).T),
        "conv_w": f(i["L1_conv_conv_w"]),
        "conv_b": cols(i["L1_conv_conv_b"]),
        "wxp": lay,
        "wdt_t": f(np.asarray(i["L1_conv_W_dt"]).T),
        "b_dt": cols(i["L1_conv_b_dt"]),
        "a_log": f(i["L1_conv_A_log"]),
        "d_skip": cols(i["L1_conv_D_skip"]),
        "wout_t": f(np.asarray(i["L1_conv_W_out"]).T),
        "ln_w": f(i["L1_conv_ln_w"])[None, :],
        "ident_d": np.eye(P, dtype=np.float32),
        "gavg_d": np.kron(np.eye(P // 8), np.full((8, 8), 0.125)).astype(np.float32),
    }


def kernel(**inputs):
    import numpy as np
    import concourse.bacc as bacc
    from concourse.bass_utils import run_bass_kernel_spmd as run

    nc = bacc.Bacc("TRN2", target_bir_lowering=False, num_devices=1)
    arrays = _arrays(inputs)
    aps = [nc.dram_tensor(name, a.shape, mybir.dt.from_np(a.dtype), kind="ExternalInput").ap()
           for name, a in arrays.items()]
    out = nc.dram_tensor("out", arrays["x"].shape, F32, kind="ExternalOutput").ap()
    build(nc, *aps, out)
    return run(nc, [arrays], core_ids=[0]).results[0]["out"]
```

```python
import concourse.bass as bass
from concourse import mybir
from contextlib import ExitStack

F32 = mybir.dt.float32
BF16 = mybir.dt.bfloat16
ALU = mybir.AluOpType
ACT = mybir.ActivationFunctionType
AX = mybir.AxisListType

P = 128
T = 64
J = 64
C = 256
CC = C // P
DI = 512
DK = DI // P
NS = 16
TAPS = 4
R = 16
TOK = T * J
GT = 512
GJ = GT // T
NG = TOK // GT
TILES = TOK // P
GTILES = GT // P
UNITS = NS * DK
BIG_DT = 1.0e25
MIN_A = 1.0e-22

XC_PE = (0, 2, 12, 15)
CONV_PE = (4, 8, 17, 21)
Z_PE = (28, 30, 35, 39)
XD_PE = 31
DT_PE = (37, 42, 47, 50)
OUT_PE = (43, 51, 55, 59)
OUT_BANK = (1, 1, 0, 1)
XC_ACT = (5, 7, 18, 20)
CONV_ACT = (11, 16, 27, 30)
SILU_ACT = 31
Z_ACT = (32, 33, 40, 44)
XD_ACT = 38
DT_ACT = (41, 46, 51, 56)
OUT_SQUARE = (49, 57, 60, 63)
OUT_LN = (50, 58, 61, 63)
OUT_EXP = (51, 59, 62, 63)
DT_DVE = (42, 47, 52, 57)
RT_DVE = 31
OUT_DVE = (50, 58, 62, 63)
DT_POOL = (47, 52, 57, 62)
U_POOL = (49, 55, 59, 63)
GATE_POOL = (2, 4, 6, 8)


def part(starts, v, parts):
    for i, first in enumerate(starts):
        if first <= v < first + parts:
            return i, v - first
    return None, None


def steps(units, v):
    return [i for i, u in enumerate(units) if u == v]


X_ORDER = (0, 1, 4, 5, 2, 3, 6, 7)
PRODS = 8

H_CREDIT = 4
PROD_CREDIT = 2
SUM_CREDIT = PRODS
OUT_CREDIT = 1
STORE_CREDIT = 32
DVE_LINKS = 21


def build(nc, x, w123, b123, win_t, conv_w, conv_b, wxp, wdt_t, b_dt, a_log, d_skip, wout_t, ln_w,
          ident_d, gavg_d, out):
    NB = x.shape[0]
    bc_rows = nc.dram_tensor("bc_rows", (2, 2 * NS, GT), F32, kind="Internal").ap()
    ctx = ExitStack()
    with ctx:
        def sb(name, shape, dt=F32):
            return ctx.enter_context(nc.sbuf_tensor(name, shape, dt))

        def sem(name):
            return ctx.enter_context(nc.semaphore(name))

        ident = sb("ident", [P, P])
        gavg = sb("gavg", [P, P])
        w3 = sb("w3", [P, CC, 3])
        b3 = sb("b3", [P, 3])
        win = sb("win", [P, CC, 2 * DI])
        cw = sb("cw", [P, DK, TAPS])
        cdiag = sb("cdiag", [P, DK, TAPS, P])
        cb = sb("cb", [P, DK])
        wx = sb("wx", [P, DK, P])
        wdt = sb("wdt", [P, DI])
        bdt = sb("bdt", [P, DK])
        alog = sb("alog", [P, DK, NS])
        amat = sb("amat", [P, DK, NS])
        dsk = sb("dsk", [P, DK])
        wout = sb("wout", [P, DK, C])
        lnw = sb("lnw", [P, C])

        xT = sb("xT", [P, CC, TOK])

        arena = sb("arena", [P, 111 * 256])
        place = [0]

        def take(n):
            place[0] += n
            assert place[0] <= arena.shape[1]
            return arena[:, place[0] - n:place[0]]

        dt_sb = take(2 * DI * GT // P).rearrange("p (q k n) -> p q k n", q=2, k=DK)
        u_sb = take(2 * DI * GT // P).rearrange("p (q k n) -> p q k n", q=2, k=DK)
        xc_sb = take(2 * DI * GT // P).rearrange("p (q k n) -> p q k n", q=2, k=DK)
        zs_sb = take(2 * DI * GT // P).rearrange("p (q k n) -> p q k n", q=2, k=DK)
        bc = take(8 * GT).rearrange("p (q i n) -> p q i n", q=4, i=2)
        yg = take(DK * GT).rearrange("p (k n) -> p k n", k=DK)
        g2 = take(CC * GT).rearrange("p (c n) -> p c n", c=CC)
        rt = take(CC * GT).rearrange("p (c n) -> p c n", c=CC)
        te = take(2 * GT).rearrange("p (q n) -> p q n", q=2)
        tl = take(2 * GT).rearrange("p (q n) -> p q n", q=2)
        tc = take(2 * GT).rearrange("p (q n) -> p q n", q=2)
        xd = take(GT)
        place[0] = 0
        ee = take(2 * TOK).rearrange("p (q n) -> p q n", q=2)
        gT = take(CC * TOK).rearrange("p (c n) -> p c n", c=CC)
        x0b = take(TOK)
        x2b = take(TOK)
        place[0] = 0
        xin = take(NG * GTILES * C).rearrange("p (g m c) -> p g m c", g=NG, m=GTILES)

        drive = sb("drive", [P, 2, 2, GT])
        prod = sb("prod", [P, PRODS, GT])
        raw = sb("raw", [P, 2, GJ, TAPS - 1 + T])
        osb = sb("osb", [P, GTILES, C])

        stats = sb("stats", [P, CC, NG, 6])
        mv = sb("mv", [P, CC, 2])
        gs = sb("gs", [P, 2 * CC])
        dev = sb("dev", [P, CC])
        gvar = sb("gvar", [P, CC])
        lnv = sb("lnv", [P, CC])
        y0 = sb("y0", [P, CC])
        nt = sb("nt", [P, 3, CC])
        gn = sb("gn", [P, 2, CC])
        rp1 = sb("rp1", [P, CC])
        x1c = sb("x1c", [P, TILES])
        mxs = sb("mxs", [P, 2, NG])
        mm = sb("mm", [P, 2])
        nm = sb("nm", [P, 3, TILES])
        den = sb("den", [P, TILES])
        num = sb("num", [P, TILES])
        gt4 = sb("gt4", [P, 5, TILES])
        ssq = sb("ssq", [P, GTILES])
        lms = sb("lms", [P, GTILES])
        rms = sb("rms", [P, GTILES])
        sqj = sb("sqj", [P, C])
        eps = sb("eps", [P, 1])
        half_big = sb("half_big", [P, GJ, 1])
        spare = sb("spare", [P, 8])

        psum = ctx.enter_context(nc.psum_tensor("psum", [P, 8, GT], F32))
        ybank = psum[:, 0:DK, :]
        hbank = psum[:, 4:6, :]
        pbank = psum[:, 6:8, :]
        abank = psum[:, 6, :]

        s_w = sem("weights_loaded")
        s_pad = sem("wdt_zeroed")
        s_init = sem("dve_ready")
        s_aexp = sem("a_exponentiated")
        s_wready = sem("weights_ready")
        s_xl = [sem(f"x_loaded{c}") for c in range(NG)]
        s_xtf = sem("xt_full")
        s_xtd = sem("xt_done")
        s_mv = sem("moments_ready")
        s_gm = sem("group_means")
        s_dev = sem("deviations")
        s_gd = sem("group_deviations")
        s_var = sem("variances")
        s_ln = sem("act_logs")
        s_y0 = sem("rstd_guess")
        s_gt = sem("gt_ready")
        s_x1f = sem("x1_full")
        s_x1d = sem("x1_done")
        s_x0f = sem("x0_full")
        s_x0d = sem("x0_done")
        s_x2f = sem("x2_full")
        s_x2d = sem("x2_done")
        s_nm = sem("negmax_ready")
        s_e = sem("e_ready")
        s_eu = sem("e_used")
        s_f = sem("feats_ready")
        s_sg = sem("gate_exp")
        s_gate = sem("gate_ready")
        s_gbf = sem("gate_bcast_full")
        s_gx = sem("gate_times_g")
        s_r1 = sem("r1_ready")
        s_g2 = sem("g2_ready")
        s_rt = sem("residual_ready")
        s_xcf = sem("xc_full")
        s_raw = sem("raw_done")
        s_cvf = sem("conv_full")
        s_cvd = sem("conv_done")
        s_zf = sem("z_full")
        s_zd = sem("z_done")
        s_silu = sem("xc_silu_done")
        s_zsilu = sem("z_silu_done")
        s_xdf = sem("xd_full")
        s_xdd = sem("xd_done")
        s_rows = sem("bc_rows_stored")
        s_dtf = sem("dt_full")
        s_dtm = sem("dt_evacuated")
        s_de = sem("dt_exp")
        s_dl = sem("dt_log")
        s_corr = sem("dt_corrected")
        s_dt = sem("dt_ready")
        s_u = sem("u_ready")
        s_dtz = sem("dt_first_steps")
        s_bc = [sem(f"bc_loaded{i}") for i in range(4)]
        s_da = sem("decay_ready")
        s_db = sem("drive_ready")
        s_h = sem("h_ready")
        s_pr = sem("prod_ready")
        s_sum = sem("sum_done")
        s_gy = sem("y_gated")
        s_yg = sem("yg_ready")
        s_of = sem("out_full")
        s_sq = sem("square_done")
        s_on = sem("out_normed")
        s_od = sem("out_done")
        s_st = sem("stored")
        s_bn = sem("bn_stats_done")
        s_dch = sem("dve_chain")

        def bc_there(eng, n, s):
            eng.wait_ge(s_bc[s % 4], n * (16 * NS // 4) + (16 * (s // 4) + 16))

        def seq(t4):
            return t4.rearrange("p (j t) -> p j t", t=T)

        block = ctx.enter_context(nc.Block())

        @block.sync
        def _(sp):
            def rows(n, q):
                sp.wait_ge(s_xdd, n + 1)
                sp.dma_start(bc_rows[q], xd[0:2 * NS, :]).then_inc(s_rows, 16)

            def bcast(n, q, s, fresh):
                if s == 0:
                    sp.wait_ge(s_rows, n * 16 + 16)
                if not fresh:
                    sp.wait_ge(s_pr, n * UNITS + (4 * s - 12 + PROD_CREDIT))
                sp.dma_start(bc[:, s % 4, :, :].rearrange("p i n -> p (i n)"),
                             bc_rows[q, 2 * s:2 * s + 2, :].rearrange("(o i) n -> o (i n)", o=1).to_broadcast([P, 2 * GT])
                             ).then_inc(s_bc[s % 4], 16)

            def step(n, q, g, proj):
                for s in range(NS):
                    if s + 2 < NS:
                        bcast(n, q, s + 2, g == 0 and s < 2)
                    elif proj:
                        if s + 2 == NS:
                            rows(n + 1, 1 - q)
                        bcast(n + 1, 1 - q, s + 2 - NS, False)

            def store(ob, n, j0):
                sp.wait_ge(s_od, n * GTILES + (GTILES + OUT_CREDIT))
                for jj in range(2):
                    sp.dma_start(ob[:, strided(j0, jj), :], osb[64 * jj:64 * jj + 64, :, :]).then_inc(s_st, 16)

            def strided(j0, jj):
                if isinstance(j0, int):
                    return slice(j0 + jj, j0 + GJ, 2)
                return bass.ds(j0 + jj, GTILES, 2)

            for dst, src in ((ident[:], ident_d), (gavg[:], gavg_d), 
                             (w3[:], w123.rearrange("(c p) i -> p c i", p=P)),
                             (b3[:], b123.to_broadcast([P, 3])),
                             (win[:], win_t.rearrange("(c p) n -> p c n", p=P)),
                             (cw[:], conv_w.rearrange("(k p) i -> p k i", p=P)),
                             (cb[:], conv_b),
                             (wx[:], wxp.rearrange("(k p) n -> p k n", p=P)),
                             (bdt[:], b_dt),
                             (alog[:], a_log.rearrange("(k p) s -> p k s", p=P)),
                             (dsk[:], d_skip),
                             (wout[:], wout_t.rearrange("(k p) n -> p k n", p=P)),
                             (lnw[:], ln_w.to_broadcast([P, C]))):
                sp.dma_start(dst, src).then_inc(s_w, 16)
            sp.wait_ge(s_pad, 1)
            sp.dma_start(wdt[32:32 + R, :], wdt_t).then_inc(s_w, 16)
            def of_batch(tensor, b):
                part = tensor[b:b + 1] if isinstance(b, int) else tensor[bass.ds(b, 1)]
                return part.rearrange("o t j c -> (o t) j c")

            def load_x(b, chunks):
                for c in chunks:
                    for jj in range(2):
                        sp.dma_start(xin[64 * jj:64 * jj + 64, c, :, :],
                                     of_batch(x, b)[:, GJ * c + jj:GJ * (c + 1):2, :]).then_inc(s_xl[c], 16)

            def batch(b, last):
                n0 = b * NG
                ob = of_batch(out, b)
                rows(n0, 0)
                bcast(n0, 0, 0, True)
                bcast(n0, 0, 1, True)
                step(n0, 0, 0, True)
                with sp.Fori(0, NG // 2 - 1) as p:
                    n = n0 + 2 * p
                    j0 = 2 * GJ * p
                    step(n + 1, 1, None, True)
                    store(ob, n, j0)
                    step(n + 2, 0, None, True)
                    store(ob, n + 1, j0 + GJ)
                step(n0 + (NG - 1), 1, NG - 1, False)
                if not last:
                    sp.wait_ge(s_h, (n0 + (NG - 1)) * UNITS + H_CREDIT)
                    load_x(b + 1, X_ORDER[:4])
                store(ob, n0 + (NG - 2), GJ * (NG - 2))
                if not last:
                    sp.wait_ge(s_h, (n0 + NG) * UNITS + H_CREDIT)
                    load_x(b + 1, X_ORDER[4:])
                store(ob, n0 + (NG - 1), GJ * (NG - 1))

            load_x(0, X_ORDER)
            if NB > 1:
                with sp.Fori(0, NB - 1) as b:
                    batch(b, False)
            batch(NB - 1, True)
            sp.wait_ge(s_st, STORE_CREDIT + NB * NG * 32)

        @block.tensor
        def _(pe):
            def layer0(b):
                for q, (c, h) in enumerate((c, h) for c in X_ORDER for h in range(CC)):
                    if h == 0:
                        pe.wait_ge(s_xl[c], b * 32 + 32)
                    if q >= 4:
                        pe.wait_ge(s_xtd, b * (NG * CC) + (q - 3))
                    for m in range(GTILES):
                        last = nc.tensor.transpose(psum[:, q % 4, m * P:(m + 1) * P],
                                                   xin[:, c, m, h * P:(h + 1) * P], ident[:])
                        if m == GTILES - 1:
                            last.then_inc(s_xtf, 1)
                group_stats(b, 0)
                for c in range(NG):
                    for h in range(CC):
                        pe.wait_ge(s_gt, b * (NG * CC) + (CC * c + h + 1))
                    if c == 0:
                        pe.wait_ge(s_xtd, (b + 1) * (NG * CC))
                    if c >= 2:
                        pe.wait_ge(s_x1d, b * NG + (c - 1))
                    for m in range(GTILES):
                        for h in range(CC):
                            last = nc.tensor.matmul(psum[:, 6 + c % 2, m * P:(m + 1) * P],
                                                    gT[:, h, (GTILES * c + m) * P:(GTILES * c + m + 1) * P],
                                                    w3[:, h, 1:2].to_broadcast([P, P]),
                                                    start=(h == 0), stop=(h == CC - 1))
                    last.then_inc(s_x1f, 1)
                    for which, full, done in ((0, s_x0f, s_x0d), (2, s_x2f, s_x2d)):
                        if c >= 2:
                            pe.wait_ge(done, b * NG + (c - 1))
                        for h in range(CC):
                            last = nc.tensor.matmul(psum[:, which + c % 2, :],
                                                    w3[:, h, which:which + 1].to_broadcast([P, P]),
                                                    gT[:, h, c * GT:(c + 1) * GT],
                                                    start=(h == 0), stop=(h == CC - 1))
                        last.then_inc(full, 1)
                pe.wait_ge(s_gate, b + 1)
                for c in range(NG):
                    if c >= 4:
                        pe.wait_ge(s_gx, b * (NG * CC) + CC * (c - 3))
                    for m in range(GTILES):
                        i = GTILES * c + m
                        last = nc.tensor.matmul(psum[:, c % 4, m * P:(m + 1) * P],
                                                gt4[:, 4, i:i + 1].to_broadcast([P, P]), ident[:],
                                                start=True, stop=True)
                    last.then_inc(s_gbf, 1)
                group_stats(b, 1)

            def group_stats(b, layer):
                pe.wait_ge(s_mv, 2 * b + (layer + 1))
                nc.tensor.matmul(abank[:, 0:4], gavg[:], mv[:, :, :].rearrange("p c i -> p (c i)"),
                                 start=True, stop=True).then_inc(s_gm, 1)
                pe.wait_ge(s_dev, 2 * b + (layer + 1))
                nc.tensor.matmul(abank[:, 8:10], gavg[:], dev[:], start=True, stop=True).then_inc(s_gd, 1)

            def project(v, n, q, g):
                i, h = part(XC_PE, v, CC)
                if i is not None:
                    if i == 0 and h == 0:
                        pe.wait_ge(s_g2, n + 1)
                        if g != 0:
                            pe.wait_ge(s_dtm, n * DK)
                            pe.wait_ge(s_zd, n * DK)
                        if g not in (0, 1, 2):
                            pe.wait_ge(s_od, (n - 2) * GTILES + OUT_CREDIT)
                    if i >= 2 and h == 0:
                        pe.wait_ge(s_cvd, n * DK + (i - 1))
                    mm = nc.tensor.matmul(pbank[:, i % 2, :], win[:, h, i * P:(i + 1) * P], g2[:, h, :],
                                          start=(h == 0), stop=(h == CC - 1))
                    if h == CC - 1:
                        mm.then_inc(s_xcf, 1)
                i, tap = part(CONV_PE, v, TAPS)
                if i is not None:
                    if tap == 0:
                        pe.wait_ge(s_raw, n * DK + (i + 1))
                    mm = nc.tensor.matmul(seq(pbank[:, i % 2, :]), cdiag[:, i, tap, :],
                                          raw[:, i % 2, :, tap:tap + T], start=(tap == 0),
                                          stop=(tap == TAPS - 1))
                    if tap == TAPS - 1:
                        mm.then_inc(s_cvf, 1)
                i, h = part(Z_PE, v, CC)
                if i is not None:
                    if h == 0 and i < 2:
                        pe.wait_ge(s_cvd, n * DK + (3 + i))
                    elif h == 0:
                        pe.wait_ge(s_zd, n * DK + i)
                    mm = nc.tensor.matmul(pbank[:, min(i, 1), :], win[:, h, DI + i * P:DI + (i + 1) * P],
                                          g2[:, h, :], start=(h == 0), stop=(h == CC - 1))
                    if h == CC - 1:
                        mm.then_inc(s_zf, 1)
                if XD_PE <= v < XD_PE + DK:
                    k = v - XD_PE
                    if k == 0:
                        pe.wait_ge(s_zd, n * DK + 1)
                        pe.wait_ge(s_silu, n + 1)
                    mm = nc.tensor.matmul(pbank[:, 0, :], wx[:, k, :], xc_sb[:, q, k, :],
                                          start=(k == 0), stop=(k == DK - 1))
                    if k == DK - 1:
                        mm.then_inc(s_xdf, 1)
                for i in steps(DT_PE, v):
                    if i == 0:
                        pe.wait_ge(s_xdd, n + 1)
                    else:
                        pe.wait_ge(s_dtm, n * DK + i)
                    nc.tensor.matmul(pbank[:, 0, :], wdt[:, i * P:(i + 1) * P], xd, start=True,
                                     stop=True).then_inc(s_dtf, 1)

            def output(v, n, proj):
                i, third = part(OUT_PE, v, 3)
                if i is None:
                    return
                bank = pbank[:, OUT_BANK[i], :]
                if third == 0:
                    if i == 0:
                        pe.wait_ge(s_yg, n * DK + DK)
                        pe.wait_ge(s_rt, n + 1)
                    if i == 0 and proj:
                        pe.wait_ge(s_zd, (n + 2) * DK + DK)
                    elif i == 2 and proj:
                        pe.wait_ge(s_dtm, (n + 2) * DK + DK)
                    elif i in (1, 3):
                        pe.wait_ge(s_od, n * GTILES + ((1, 2)[i // 2] + OUT_CREDIT))
                if third < 2:
                    for k in (2 * third, 2 * third + 1):
                        nc.tensor.matmul(bank[:, 0:C], yg[:, k, i * P:(i + 1) * P], wout[:, k, :],
                                         start=(k == 0), stop=(k == DK - 1))
                else:
                    for h in range(CC):
                        last = nc.tensor.transpose(bank[:, C + h * P:C + (h + 1) * P],
                                                   rt[:, h, i * P:(i + 1) * P], ident[:])
                    last.then_inc(s_of, 1)

            def output_last(n):
                pe.wait_ge(s_od, n * GTILES + OUT_CREDIT)
                pe.wait_ge(s_rt, n + 1)
                for k in range(DK):
                    pe.wait_ge(s_yg, n * DK + (k + 1))
                    for i in range(GTILES):
                        nc.tensor.matmul(psum[:, 4 + i, 0:C], yg[:, k, i * P:(i + 1) * P], wout[:, k, :],
                                         start=(k == 0), stop=(k == DK - 1))
                        if k == DK - 1:
                            for h in range(CC):
                                last = nc.tensor.transpose(psum[:, 4 + i, C + h * P:C + (h + 1) * P],
                                                           rt[:, h, i * P:(i + 1) * P], ident[:])
                            last.then_inc(s_of, 1)

            def step(n, q, g, proj, outp):
                for v in range(UNITS):
                    s, k = divmod(v, DK)
                    pe.wait_ge(s_pr, n * UNITS + (v + 1 + PROD_CREDIT))
                    if s == 0 and g != 0:
                        pe.wait_ge(s_gy, n * DK + (k + 1 - DK))
                    nc.tensor.matmul(ybank[:, k, :], ident[:], prod[:, v % PRODS, :], start=(s == 0),
                                     stop=(s == NS - 1)).then_inc(s_sum, 1)
                    if proj:
                        project(v, n + 1, 1 - q, -1 if g is None else g + 1)
                    if outp:
                        output(v, n - 1, proj)

            pe.wait_ge(s_w, 16 * 14)
            pe.wait_ge(s_wready, 1)
            with pe.Fori(0, NB) as b:
                n0 = b * NG
                layer0(b)
                for v in range(UNITS):
                    project(v, n0, 0, 0)
                step(n0, 0, 0, True, False)
                with pe.Fori(0, NG // 2 - 1) as p:
                    n = n0 + 2 * p
                    step(n + 1, 1, None, True, True)
                    step(n + 2, 0, None, True, True)
                step(n0 + (NG - 1), 1, NG - 1, False, True)
                output_last(n0 + (NG - 1))
                pe.wait_ge(s_od, (b + 1) * (NG * GTILES) + OUT_CREDIT)

        @block.scalar
        def _(act):
            def exp_ln_table():
                nc.scalar.preload_act_table_set("natural_log_exp_and_others")

            def group_stats(b, layer):
                act.wait_ge(s_var, 2 * b + (layer + 1))
                nc.scalar.activation(lnv[:], gvar[:], ACT.Ln).then_inc(s_ln, 1)
                act.wait_ge(s_ln, 2 * b + (layer + 1))
                nc.scalar.activation(y0[:], lnv[:], ACT.Exp, scale=-0.5).then_inc(s_y0, 1)

            def layer0(b):
                for q, (c, h) in enumerate((c, h) for c in X_ORDER for h in range(CC)):
                    act.wait_ge(s_xtf, b * (NG * CC) + (q + 1))
                    nc.scalar.activation(xT[:, h, c * GT:(c + 1) * GT], psum[:, q % 4, :],
                                         ACT.Copy).then_inc(s_xtd, 1)
                group_stats(b, 0)
                for c in range(NG):
                    act.wait_ge(s_x0f, b * NG + (c + 1))
                    nc.scalar.activation(x0b[:, c * GT:(c + 1) * GT], psum[:, c % 2, :], ACT.Identity,
                                         bias=b3[:, 0:1]).then_inc(s_x0d, 1)
                act.wait_ge(s_nm, b + 1)
                act.wait_ge(s_x0d, b * NG + NG)
                for i in range(TILES):
                    if i >= 2:
                        act.wait_ge(s_eu, b * TILES + (i - 1))
                    nc.scalar.activation(ee[:, i % 2, :], x0b, ACT.Exp, bias=nm[:, 2, i:i + 1],
                                         scale=x1c[:, i:i + 1], accum_out=den[:, i:i + 1]).then_inc(s_e, 1)
                act.wait_ge(s_f, b + 1)
                nc.scalar.activation(gt4[:, 2, :], gt4[:, 1, :], ACT.Exp, scale=-1.0).then_inc(s_sg, 1)
                group_stats(b, 1)

            def project(v, n, q, first, prologue):
                for i in steps(CONV_ACT, v):
                    act.wait_ge(s_cvf, n * DK + (i + 1))
                    if i == 0 and not first:
                        act.wait_ge(s_gy, (n - 1) * DK)
                    nc.scalar.activation(xc_sb[:, q, i, :], pbank[:, i % 2, :], ACT.Identity,
                                         bias=cb[:, i:i + 1]).then_inc(s_cvd, 1)
                for i in steps(XC_ACT, v):
                    act.wait_ge(s_xcf, n * DK + (i + 1))
                    if i >= 2:
                        act.wait_ge(s_cvf, n * DK + (i - 1))
                    nc.scalar.activation(raw[:, i % 2, :, TAPS - 1:], seq(pbank[:, i % 2, :]),
                                         ACT.Copy).then_inc(s_raw, 1)
                for i in steps(Z_ACT, v):
                    act.wait_ge(s_zf, n * DK + (i + 1))
                    if i == 0 and not first:
                        act.wait_ge(s_yg, (n - 1) * DK)
                    nc.scalar.activation(zs_sb[:, q, i, :], pbank[:, min(i, 1), :], ACT.Copy).then_inc(s_zd, 1)
                if v == XD_ACT:
                    act.wait_ge(s_xdf, n + 1)
                    nc.scalar.activation(xd, pbank[:, 0, :], ACT.Copy).then_inc(s_xdd, 1)
                for i in steps(DT_ACT, v):
                    act.wait_ge(s_dtf, n * DK + (i + 1))
                    if not (prologue and i < 2):
                        act.wait_ge(s_corr, n * (3 * DK) + 3 * (i - 1))
                    nc.scalar.activation(te[:, i % 2, :], pbank[:, 0, :], ACT.Abs, bias=bdt[:, i:i + 1])
                    nc.scalar.activation(dt_sb[:, q, i, :], pbank[:, 0, :], ACT.Relu,
                                         bias=bdt[:, i:i + 1]).then_inc(s_dtm, 1)
                for i in steps(DT_ACT, v - 1):
                    act.wait_ge(s_dtm, n * DK + (i + 1))
                    nc.scalar.activation(te[:, i % 2, :], te[:, i % 2, :], ACT.Exp, scale=-1.0).then_inc(s_de, 1)
                for i in steps(DT_ACT, v - 2):
                    act.wait_ge(s_de, n * DK + (i + 1))
                    nc.scalar.activation(tl[:, i % 2, :], te[:, i % 2, :], ACT.Ln, bias=1.0).then_inc(s_dl, 1)

            def silu(n_xc, q_xc, n_z, q_z):
                if n_xc is not None:
                    act.wait_ge(s_cvd, n_xc * DK + DK)
                    nc.scalar.activation(xc_sb[:, q_xc, :, :], xc_sb[:, q_xc, :, :], ACT.Silu).then_inc(s_silu, 1)
                if n_z is not None:
                    act.wait_ge(s_zd, n_z * DK + DK)
                    nc.scalar.activation(zs_sb[:, q_z, :, :], zs_sb[:, q_z, :, :], ACT.Silu).then_inc(s_zsilu, 1)
                exp_ln_table()

            def square(i, n, bank):
                act.wait_ge(s_of, n * GTILES + (i + 1))
                nc.scalar.activation(sqj[:], bank[:, 0:C], ACT.Square, accum_out=ssq[:, i:i + 1]).then_inc(s_sq, 1)

            def log_mean(i, n):
                act.wait_ge(s_sq, n * (3 * GTILES) + (3 * i + 1))
                nc.scalar.activation(lms[:, i:i + 1], ssq[:, i:i + 1], ACT.Ln, scale=1.0 / C,
                                     bias=eps[:, 0:1]).then_inc(s_sq, 1)

            def inv_root(i, n):
                act.wait_ge(s_sq, n * (3 * GTILES) + (3 * i + 2))
                nc.scalar.activation(rms[:, i:i + 1], lms[:, i:i + 1], ACT.Exp, scale=-0.5).then_inc(s_sq, 1)

            def output(v, n):
                for i in range(GTILES):
                    if v == OUT_SQUARE[i]:
                        square(i, n, pbank[:, OUT_BANK[i], :])
                    if v == OUT_LN[i]:
                        log_mean(i, n)
                    if v == OUT_EXP[i]:
                        inv_root(i, n)

            def step(n, q, g, proj, outp):
                for v in range(UNITS):
                    s, k = divmod(v, DK)
                    if s == 0:
                        act.wait_ge(s_dtz, n * DK + (k + 1))
                    act.wait_ge(s_pr, n * UNITS + (v - 1 + PROD_CREDIT))
                    nc.scalar.activation(hbank[:, v % 2, :], dt_sb[:, q, k, :], ACT.Exp,
                                         scale=amat[:, k, s:s + 1]).then_inc(s_da, 1)
                    if proj:
                        project(v, n + 1, 1 - q, g == 0, False)
                    if v == SILU_ACT:
                        silu(n + 1 if proj else None, 1 - q, n, q)
                    if outp:
                        output(v, n - 1)

            act.wait_ge(s_w, 16 * 14)
            nc.scalar.activation(amat[:], alog[:], ACT.Exp).then_inc(s_aexp, 1)
            act.wait_ge(s_wready, 1)
            with act.Fori(0, NB) as b:
                n0 = b * NG
                exp_ln_table()
                layer0(b)
                for v in range(UNITS):
                    project(v, n0, 0, True, True)
                    if v == SILU_ACT:
                        silu(n0, 0, None, None)
                step(n0, 0, 0, True, False)
                with act.Fori(0, NG // 2 - 1) as p:
                    n = n0 + 2 * p
                    exp_ln_table()
                    step(n + 1, 1, None, True, True)
                    step(n + 2, 0, None, True, True)
                exp_ln_table()
                step(n0 + (NG - 1), 1, NG - 1, False, True)
                for i in range(GTILES):
                    square(i, n0 + (NG - 1), psum[:, 4 + i, :])
                    log_mean(i, n0 + (NG - 1))
                    inv_root(i, n0 + (NG - 1))
                act.wait_ge(s_of, (b + 1) * (NG * GTILES))

        @block.gpsimd
        def _(pool):
            def project(v, n, q):
                for i in steps(DT_POOL, v):
                    pool.wait_ge(s_corr, n * (3 * DK) + (3 * i + 3))
                    nc.gpsimd.tensor_tensor(dt_sb[:, q, i, :], dt_sb[:, q, i, :], tc[:, i % 2, :],
                                            ALU.add).then_inc(s_dt, 1)
                for i in steps(U_POOL, v):
                    pool.wait_ge(s_dt, n * DK + (i + 1))
                    nc.gpsimd.tensor_tensor(u_sb[:, q, i, :], dt_sb[:, q, i, :], xc_sb[:, q, i, :],
                                            ALU.mult).then_inc(s_u, 1)
                    pool.wait_ge(s_u, n * DK + (i + 1))
                    nc.gpsimd.tensor_tensor(seq(dt_sb[:, q, i, :])[:, :, 0:1], half_big[:], half_big[:],
                                            ALU.add).then_inc(s_dtz, 1)

            def gate(n, q, k):
                pool.wait_ge(s_zsilu, n + 1)
                pool.wait_ge(s_gy, n * DK + (k + 1))
                nc.gpsimd.tensor_tensor(yg[:, k, :], yg[:, k, :], zs_sb[:, q, k, :], ALU.mult).then_inc(s_yg, 1)

            def step(n, q, proj, gate_prev):
                for v in range(0, UNITS, 2):
                    s, k = divmod(v, DK)
                    if s == 0:
                        pool.wait_ge(s_u, n * DK + (k + 2))
                    bc_there(pool, n, s)
                    pool.wait_ge(s_h, n * UNITS + (v - 2 + H_CREDIT))
                    nc.gpsimd.tensor_tensor(drive[:, (v // 2) % 2, :, :], u_sb[:, q, k:k + 2, :],
                                            bc[:, s % 4, 0:1, :].to_broadcast([P, 2, GT]),
                                            ALU.mult).then_inc(s_db, 1)
                    if gate_prev:
                        for kg in steps(GATE_POOL, v):
                            gate(n - 1, 1 - q, kg)
                    if proj:
                        for w in (v, v + 1):
                            project(w, n + 1, 1 - q)

            with pool.Fori(0, NB) as b:
                n0 = b * NG
                for c in range(NG):
                    for h in range(CC):
                        pool.wait_ge(s_gx, b * (NG * CC) + (CC * c + h + 1))
                        nc.gpsimd.tensor_tensor(xT[:, h, c * GT:(c + 1) * GT], xT[:, h, c * GT:(c + 1) * GT],
                                                gT[:, h, c * GT:(c + 1) * GT], ALU.add).then_inc(s_r1, 1)
                for v in range(UNITS):
                    project(v, n0, 0)
                step(n0, 0, True, False)
                with pool.Fori(0, NG // 2 - 1) as p:
                    n = n0 + 2 * p
                    step(n + 1, 1, True, True)
                    step(n + 2, 0, True, True)
                step(n0 + (NG - 1), 1, False, True)
                for k in range(DK):
                    gate(n0 + (NG - 1), 1, k)

        @block.vector
        def _(dve):
            def group_stats(b, layer):
                dve.wait_ge(s_bn, b * (2 * NG * CC) + (layer + 1) * NG * CC)
                nc.vector.tensor_copy(spare[:, 7:8], stats[:, 0, 0, 0:1])
                for h in range(CC):
                    last = nc.vector.bn_aggr(mv[:, h, :], stats[:, h, :, :].rearrange("p c i -> p (c i)"))
                last.then_inc(s_mv, 1)
                dve.wait_ge(s_gm, 2 * b + (layer + 1))
                link(b, nc.vector.tensor_copy(gs[:], abank[:, 0:4]))
                gsv = gs[:].rearrange("p (c i) -> p c i", c=CC)
                link(b, nc.vector.tensor_tensor(nt[:, 0, :], mv[:, :, 0], gsv[:, :, 0], ALU.subtract))
                nc.vector.tensor_tensor(dev[:], nt[:, 0, :], nt[:, 0, :], ALU.mult).then_inc(s_dev, 1)
                dve.wait_ge(s_gd, 2 * b + (layer + 1))
                nc.vector.scalar_tensor_tensor(out=gvar[:], in0=abank[:, 8:10], scalar=1e-5, in1=gsv[:, :, 1],
                                               op0=ALU.add, op1=ALU.add).then_inc(s_var, 1)
                dve.wait_ge(s_y0, 2 * b + (layer + 1))
                link(b, nc.vector.tensor_tensor(nt[:, 0, :], y0[:], y0[:], ALU.mult))
                link(b, nc.vector.tensor_tensor(nt[:, 1, :], nt[:, 0, :], gvar[:], ALU.mult))
                link(b, nc.vector.tensor_scalar(nt[:, 0, :], nt[:, 1, :], -0.5, 1.5, ALU.mult, ALU.add))
                link(b, nc.vector.tensor_tensor(gn[:, 0, :], y0[:], nt[:, 0, :], ALU.mult))
                link(b, nc.vector.scalar_tensor_tensor(out=gn[:, 1, :], in0=gsv[:, :, 0], scalar=-1.0,
                                                       in1=gn[:, 0, :], op0=ALU.mult, op1=ALU.mult))

            count = [0]

            def link(b, ins):
                count[0] += 1
                ins.then_inc(s_dch, 1)
                dve.wait_ge(s_dch, b * DVE_LINKS + count[0])

            def layer0(b):
                for q, (c, h) in enumerate((c, h) for c in X_ORDER for h in range(CC)):
                        dve.wait_ge(s_xtd, b * (NG * CC) + (q + 1))
                        nc.vector.bn_stats(stats[:, h, c, :], xT[:, h, c * GT:(c + 1) * GT]).then_inc(s_bn, 1)
                group_stats(b, 0)
                for c in range(NG):
                    for h in range(CC):
                        nc.vector.tensor_scalar(gT[:, h, c * GT:(c + 1) * GT], xT[:, h, c * GT:(c + 1) * GT],
                                                gn[:, 0, h:h + 1], gn[:, 1, h:h + 1], ALU.mult,
                                                ALU.add).then_inc(s_gt, 1)
                for c in range(NG):
                    dve.wait_ge(s_x1f, b * NG + (c + 1))
                    nc.vector.tensor_scalar(x1c[:, GTILES * c:GTILES * (c + 1)],
                                            psum[:, 6 + c % 2, :].rearrange("p (m n) -> p m n", n=P)[:, :, 0],
                                            b3[:, 1:2], None, ALU.add).then_inc(s_x1d, 1)
                    dve.wait_ge(s_x2f, b * NG + (c + 1))
                    nc.vector.tensor_scalar(x2b[:, c * GT:(c + 1) * GT], psum[:, 2 + c % 2, :],
                                            b3[:, 2:3], None, ALU.add).then_inc(s_x2d, 1)
                    dve.wait_ge(s_x0d, b * NG + (c + 1))
                    nc.vector.tensor_reduce(mxs[:, 0, c:c + 1], x0b[:, c * GT:(c + 1) * GT], AX.X, ALU.max)
                    last = nc.vector.tensor_reduce(mxs[:, 1, c:c + 1], x0b[:, c * GT:(c + 1) * GT], AX.X, ALU.min)
                link(b, last)
                nc.vector.tensor_reduce(mm[:, 0:1], mxs[:, 0, :], AX.X, ALU.max)
                link(b, nc.vector.tensor_reduce(mm[:, 1:2], mxs[:, 1, :], AX.X, ALU.min))
                nc.vector.tensor_scalar(nm[:, 0, :], x1c[:], mm[:, 0:1], None, ALU.mult)
                link(b, nc.vector.tensor_scalar(nm[:, 1, :], x1c[:], mm[:, 1:2], None, ALU.mult))
                link(b, nc.vector.tensor_tensor(nm[:, 0, :], nm[:, 0, :], nm[:, 1, :], ALU.max))
                nc.vector.tensor_scalar(nm[:, 2, :], nm[:, 0, :], -1.0, None, ALU.mult).then_inc(s_nm, 1)
                for i in range(TILES):
                    dve.wait_ge(s_e, b * TILES + (i + 1))
                    nc.vector.tensor_tensor_reduce(out=ee[:, i % 2, :], in0=ee[:, i % 2, :], in1=x2b, scale=1.0,
                                                   scalar=0.0, op0=ALU.mult, op1=ALU.add,
                                                   accum_out=num[:, i:i + 1]).then_inc(s_eu, 1)
                dve.wait_ge(s_eu, b * TILES + TILES)
                link(b, nc.vector.reciprocal(gt4[:, 0, :], den[:]))
                nc.vector.tensor_tensor(gt4[:, 1, :], num[:], gt4[:, 0, :], ALU.mult).then_inc(s_f, 1)
                dve.wait_ge(s_sg, b + 1)
                link(b, nc.vector.tensor_scalar(gt4[:, 3, :], gt4[:, 2, :], 1.0, None, ALU.add))
                nc.vector.reciprocal(gt4[:, 4, :], gt4[:, 3, :]).then_inc(s_gate, 1)
                for c in range(NG):
                    dve.wait_ge(s_gbf, b * NG + (c + 1))
                    for h in range(CC):
                        nc.vector.tensor_tensor(gT[:, h, c * GT:(c + 1) * GT], gT[:, h, c * GT:(c + 1) * GT],
                                                psum[:, c % 4, :], ALU.mult).then_inc(s_gx, 1)
                    if c:
                        r1_stats(b, c - 1)
                r1_stats(b, NG - 1)
                group_stats(b, 1)
                link(b, nc.vector.tensor_scalar(rp1[:], gn[:, 0, :], 1.0, None, ALU.add))

            def r1_stats(b, c):
                for h in range(CC):
                    dve.wait_ge(s_r1, b * (NG * CC) + (CC * c + h + 1))
                    nc.vector.bn_stats(stats[:, h, c, :], xT[:, h, c * GT:(c + 1) * GT]).then_inc(s_bn, 1)

            def span(g):
                return slice(g * GT, (g + 1) * GT) if isinstance(g, int) else bass.ds(g * GT, GT)

            def normalise(n, g_in_batch, first):
                if not first:
                    dve.wait_ge(s_zf, n * DK)
                for h in range(CC):
                    last = nc.vector.tensor_scalar(g2[:, h, :], xT[:, h, span(g_in_batch)],
                                                   gn[:, 0, h:h + 1], gn[:, 1, h:h + 1], ALU.mult, ALU.add)
                last.then_inc(s_g2, 1)

            def residual(n, g_in_batch):
                for h in range(CC):
                    last = nc.vector.tensor_scalar(rt[:, h, :], xT[:, h, span(g_in_batch)],
                                                   rp1[:, h:h + 1], gn[:, 1, h:h + 1], ALU.mult, ALU.add)
                last.then_inc(s_rt, 1)

            def project(v, n, first):
                i, third = part(DT_DVE, v, 3)
                if third == 0:
                    if not (first and i < 2):
                        dve.wait_ge(s_dt, n * DK + (i - 1))
                    dve.wait_ge(s_de, n * DK + (i + 1))
                    nc.vector.tensor_scalar(tc[:, i % 2, :], te[:, i % 2, :], 1.0, 1.0, ALU.add, ALU.subtract).then_inc(s_corr, 1)
                elif third == 1:
                    dve.wait_ge(s_corr, n * (3 * DK) + (3 * i + 1))
                    nc.vector.tensor_tensor(tc[:, i % 2, :], te[:, i % 2, :], tc[:, i % 2, :], ALU.subtract).then_inc(s_corr, 1)
                elif third == 2:
                    dve.wait_ge(s_dl, n * DK + (i + 1))
                    dve.wait_ge(s_corr, n * (3 * DK) + (3 * i + 2))
                    nc.vector.tensor_tensor(tc[:, i % 2, :], tl[:, i % 2, :], tc[:, i % 2, :], ALU.add).then_inc(s_corr, 1)

            def output(i, n, bank):
                dve.wait_ge(s_sq, n * (3 * GTILES) + (3 * i + 3))
                if i == 0:
                    dve.wait_ge(s_st, n * 32 + STORE_CREDIT)
                nc.vector.scalar_tensor_tensor(out=osb[:, i, :], in0=bank[:, 0:C], scalar=rms[:, i:i + 1],
                                               in1=lnw[:], op0=ALU.mult, op1=ALU.mult).then_inc(s_on, 1)
                dve.wait_ge(s_on, n * GTILES + (i + 1))
                nc.vector.tensor_tensor(osb[:, i, :], osb[:, i, :], bank[:, C:2 * C],
                                        ALU.add).then_inc(s_od, 1)

            def gate(n, q, k):
                dve.wait_ge(s_sum, n * UNITS + (UNITS - DK + k + 1 + SUM_CREDIT))
                nc.vector.scalar_tensor_tensor(out=yg[:, k, :], in0=xc_sb[:, q, k, :], scalar=dsk[:, k:k + 1],
                                               in1=ybank[:, k, :], op0=ALU.mult, op1=ALU.add).then_inc(s_gy, 1)

            def step(n, q, g_in_batch, proj, prev):
                if proj:
                    normalise(n + 1, g_in_batch + 1, False)
                for v in range(UNITS):
                    s, k = divmod(v, DK)
                    dve.wait_ge(s_da, n * UNITS + (v + 1))
                    if v % 2 == 0:
                        dve.wait_ge(s_db, n * (UNITS // 2) + (v // 2 + 1))
                    nc.vector.tensor_tensor_scan(hbank[:, v % 2, :], hbank[:, v % 2, :],
                                                 drive[:, (v // 2) % 2, v % 2, :], 0.0, ALU.mult,
                                                 ALU.add).then_inc(s_h, 1)
                    if k == 0:
                        bc_there(dve, n, s)
                    dve.wait_ge(s_sum, n * UNITS + (v + 1 - PRODS + SUM_CREDIT))
                    dve.wait_ge(s_h, n * UNITS + (v + 1 + H_CREDIT))
                    nc.vector.tensor_tensor(prod[:, v % PRODS, :], hbank[:, v % 2, :], bc[:, s % 4, 1, :],
                                            ALU.mult).then_inc(s_pr, 1)
                    if prev and v < DK:
                        gate(n - 1, 1 - q, v)
                    if proj:
                        project(v, n + 1, False)
                    if prev:
                        if v == RT_DVE:
                            residual(n - 1, g_in_batch - 1)
                        for i in steps(OUT_DVE, v):
                            output(i, n - 1, pbank[:, OUT_BANK[i], :])

            nc.vector.memset(wdt[:], 0.0).then_inc(s_pad, 1)
            nc.vector.memset(eps[:], 1e-6)
            nc.vector.memset(half_big[:], BIG_DT / 2)
            nc.vector.memset(raw[:], 0.0)
            for i, (credited, credit) in enumerate(((s_h, H_CREDIT), (s_pr, PROD_CREDIT), (s_sum, SUM_CREDIT),
                                                    (s_od, OUT_CREDIT),
                                                    (s_st, STORE_CREDIT))):
                nc.vector.memset(spare[:, i:i + 1], 0.0).then_inc(credited, credit)
            dve.wait_ge(s_w, 16 * 14)
            for k in range(DK):
                for tap in range(TAPS):
                    nc.vector.tensor_scalar(cdiag[:, k, tap, :], ident[:], cw[:, k, tap:tap + 1], None, ALU.mult)
            dve.wait_ge(s_aexp, 1)
            nc.vector.tensor_scalar(amat[:], amat[:], MIN_A, -1.0, ALU.max, ALU.mult).then_inc(s_wready, 1)
            dve.wait_ge(s_wready, 1)
            with dve.Fori(0, NB) as b:
                n0 = b * NG
                layer0(b)
                normalise(n0, 0, True)
                for v in range(UNITS):
                    project(v, n0, True)
                step(n0, 0, 0, True, False)
                with dve.Fori(0, NG // 2 - 1) as p:
                    n = n0 + 2 * p
                    step(n + 1, 1, 2 * p + 1, True, True)
                    step(n + 2, 0, 2 * p + 2, True, True)
                step(n0 + (NG - 1), 1, NG - 1, False, True)
                residual(n0 + (NG - 1), NG - 1)
                for k in range(DK):
                    gate(n0 + (NG - 1), 1, k)
                for i in range(GTILES):
                    output(i, n0 + (NG - 1), psum[:, 4 + i, :])
                assert count[0] == DVE_LINKS, count


def _arrays(i):
    import numpy as np
    f = lambda a: np.ascontiguousarray(np.asarray(a))
    cols = lambda a: f(np.asarray(a).reshape(DK, P).T)
    wxp = f(i["L1_conv_W_xproj"])
    dt_rows, bc_rows = wxp[:R], wxp[R:]
    lay = np.zeros((DI, P), np.float32)
    lay[:, 0:2 * NS:2] = bc_rows[:NS].T
    lay[:, 1:2 * NS:2] = bc_rows[NS:].T
    lay[:, 2 * NS:2 * NS + R] = dt_rows.T
    return {
        "x": f(i["x"]),
        "w123": f(np.stack([i["L0_conv_w1"], i["L0_conv_w2"], i["L0_conv_w3"]], 1)),
        "b123": f(np.concatenate([i["L0_conv_b1"], i["L0_conv_b2"], i["L0_conv_b3"]])[None, :]),
        "win_t": f(np.asarray(i["L1_conv_W_in"]).T),
        "conv_w": f(i["L1_conv_conv_w"]),
        "conv_b": cols(i["L1_conv_conv_b"]),
        "wxp": lay,
        "wdt_t": f(np.asarray(i["L1_conv_W_dt"]).T),
        "b_dt": cols(i["L1_conv_b_dt"]),
        "a_log": f(i["L1_conv_A_log"]),
        "d_skip": cols(i["L1_conv_D_skip"]),
        "wout_t": f(np.asarray(i["L1_conv_W_out"]).T),
        "ln_w": f(i["L1_conv_ln_w"])[None, :],
        "ident_d": np.eye(P, dtype=np.float32),
        "gavg_d": np.kron(np.eye(P // 8), np.full((8, 8), 0.125)).astype(np.float32),
    }


def kernel(**inputs):
    import numpy as np
    import concourse.bacc as bacc
    from concourse.bass_utils import run_bass_kernel_spmd as run

    nc = bacc.Bacc("TRN2", target_bir_lowering=False, num_devices=1)
    arrays = _arrays(inputs)
    aps = [nc.dram_tensor(name, a.shape, mybir.dt.from_np(a.dtype), kind="ExternalInput").ap()
           for name, a in arrays.items()]
    out = nc.dram_tensor("out", arrays["x"].shape, F32, kind="ExternalOutput").ap()
    build(nc, *aps, out)
    return run(nc, [arrays], core_ids=[0]).results[0]["out"]
```

```python
import concourse.bass as bass
from concourse import mybir
from contextlib import ExitStack

F32 = mybir.dt.float32
ALU = mybir.AluOpType
ACT = mybir.ActivationFunctionType
AX = mybir.AxisListType

P = 128
T = 64
J = 64
C = 256
CC = C // P
DI = 512
DK = DI // P
NS = 16
TAPS = 4
R = 16
TOK = T * J
GT = 512
GJ = GT // T
NG = TOK // GT
TILES = TOK // P
GTILES = GT // P
UNITS = NS * DK
BIG_DT = 1.0e25
MIN_A = 1.0e-22

XC_PE = (0, 2, 12, 14)
CONV_PE = (2, 8, 17, 21)
Z_PE = (29, 31, 35, 39)
XD_PE = 32
DT_PE = (37, 43, 46, 51)
OUT_PE = (43, 51, 54, 58)
OUT_BANK = (1, 1, 0, 1)
XC_ACT = (5, 7, 18, 20)
CONV_ACT = (11, 15, 28, 31)
NORM_ACT = (0, 1)
RT_ACT = (22, 25)
SILU_ACT = 32
Z_ACT = (33, 34, 41, 45)
XD_ACT = 39
DT_ACT = (42, 47, 52, 56)
OUT_SQUARE = (50, 57, 60, 63)
OUT_LN = (51, 58, 62, 63)
OUT_EXP = (51, 59, 62, 63)
DT_DVE = (43, 48, 53, 57)
OUT_DVE = (52, 59, 62, 63)
DT_POOL = (48, 53, 57, 62)
U_POOL = (50, 55, 59, 62)
GATE_POOL = (2, 2, 6, 8)


def part(starts, v, parts):
    for i, first in enumerate(starts):
        if first <= v < first + parts:
            return i, v - first
    return None, None


def steps(units, v):
    return [i for i, u in enumerate(units) if u == v]


PRODS = 8
X_ORDER = (0, 1, 4, 5, 2, 3, 6, 7)

H_CREDIT = 4
PROD_CREDIT = 2
SUM_CREDIT = PRODS
OUT_CREDIT = 1
STORE_CREDIT = 32
DVE_LINKS = 21


def build(nc, x, w123, b123, win_t, conv_w, conv_b, wxp, wdt_t, b_dt, a_log, d_skip, wout_t, ln_w,
          ident_d, gavg_d, out):
    NB = x.shape[0]
    bc_rows = nc.dram_tensor("bc_rows", (2, 2 * NS, GT), F32, kind="Internal").ap()
    x1_row = nc.dram_tensor("x1_row", (1, TOK), F32, kind="Internal").ap()
    x02_rows = nc.dram_tensor("x02_rows", (NG, 2, GT), F32, kind="Internal").ap()
    ctx = ExitStack()
    with ctx:
        def sb(name, shape, dt=F32):
            return ctx.enter_context(nc.sbuf_tensor(name, shape, dt))

        def sem(name):
            return ctx.enter_context(nc.semaphore(name))

        ident = sb("ident", [P, P])
        gavg = sb("gavg", [P, P])
        w3 = sb("w3", [P, CC, 3])
        b3 = sb("b3", [P, 1])
        win = sb("win", [P, CC, 2 * DI])
        cw = sb("cw", [P, DK, TAPS])
        cdiag = sb("cdiag", [P, DK, TAPS, P])
        cb = sb("cb", [P, DK])
        wx = sb("wx", [P, DK, P])
        wdt = sb("wdt", [P, DI])
        bdt = sb("bdt", [P, DK])
        alog = sb("alog", [P, DK, NS])
        amat = sb("amat", [P, DK, NS])
        dsk = sb("dsk", [P, DK])
        wout = sb("wout", [P, DK, C])
        lnw = sb("lnw", [P, C])

        xT = sb("xT", [P, CC, TOK])

        arena = sb("arena", [P, 111 * 256])
        place = [0]

        def take(n):
            place[0] += n
            assert place[0] <= arena.shape[1]
            return arena[:, place[0] - n:place[0]]

        dt_sb = take(2 * DI * GT // P).rearrange("p (q k n) -> p q k n", q=2, k=DK)
        u_sb = take(2 * DI * GT // P).rearrange("p (q k n) -> p q k n", q=2, k=DK)
        xc_sb = take(2 * DI * GT // P).rearrange("p (q k n) -> p q k n", q=2, k=DK)
        zs_sb = take(2 * DI * GT // P).rearrange("p (q k n) -> p q k n", q=2, k=DK)
        bc = take(8 * GT).rearrange("p (q i n) -> p q i n", q=4, i=2)
        yg = take(DK * GT).rearrange("p (k n) -> p k n", k=DK)
        g2 = take(CC * GT).rearrange("p (c n) -> p c n", c=CC)
        rt = take(CC * GT).rearrange("p (c n) -> p c n", c=CC)
        te = take(2 * GT).rearrange("p (q n) -> p q n", q=2)
        tl = take(2 * GT).rearrange("p (q n) -> p q n", q=2)
        tc = take(2 * GT).rearrange("p (q n) -> p q n", q=2)
        xd = take(GT)
        place[0] = 0
        ee = take(2 * TOK).rearrange("p (q n) -> p q n", q=2)
        gT = take(CC * TOK).rearrange("p (c n) -> p c n", c=CC)
        x02 = take(2 * TOK).rearrange("p (i n) -> p i n", i=2)
        x0b = x02[:, 0, :]
        x2b = x02[:, 1, :]
        rows3 = arena[0:3, 0:TOK]
        place[0] = 0
        xin = take(NG * GTILES * C).rearrange("p (g m c) -> p g m c", g=NG, m=GTILES)

        drive = sb("drive", [P, 2, 2, GT])
        prod = sb("prod", [P, PRODS, GT])
        raw = sb("raw", [P, 2, GJ, TAPS - 1 + T])
        osb = sb("osb", [P, GTILES, C])

        stats = sb("stats", [P, CC, NG, 6])
        mv = sb("mv", [P, CC, 2])
        gs = sb("gs", [P, 2 * CC])
        dev = sb("dev", [P, CC])
        gvar = sb("gvar", [P, CC])
        lnv = sb("lnv", [P, CC])
        y0 = sb("y0", [P, CC])
        nt = sb("nt", [P, 3, CC])
        gn = sb("gn", [P, 2, CC])
        rp1 = sb("rp1", [P, CC])
        x1c = sb("x1c", [P, TILES])
        x1t = sb("x1t", [P, P])
        mxs = sb("mxs", [P, 2, NG])
        mm = sb("mm", [P, 2])
        nm = sb("nm", [P, 3, TILES])
        den = sb("den", [P, TILES])
        num = sb("num", [P, TILES])
        gt4 = sb("gt4", [P, 5, TILES])
        ssq = sb("ssq", [P, GTILES])
        lms = sb("lms", [P, GTILES])
        rms = sb("rms", [P, GTILES])
        sqj = sb("sqj", [P, C])
        eps = sb("eps", [P, 1])
        half_big = sb("half_big", [P, GJ, 1])
        spare = sb("spare", [P, 8])

        psum = ctx.enter_context(nc.psum_tensor("psum", [P, 8, GT], F32))
        ybank = psum[:, 0:DK, :]
        hbank = psum[:, 4:6, :]
        pbank = psum[:, 6:8, :]
        abank = psum[:, 6, :]

        s_w = sem("weights_loaded")
        s_pad = sem("wdt_zeroed")
        s_aexp = sem("a_exponentiated")
        s_wready = sem("weights_ready")
        s_xl = [sem(f"x_loaded{c}") for c in range(NG)]
        s_xtf = sem("xt_full")
        s_xtd = sem("xt_done")
        s_mv = sem("moments_ready")
        s_gm = sem("group_means")
        s_dev = sem("deviations")
        s_gd = sem("group_deviations")
        s_var = sem("variances")
        s_ln = sem("act_logs")
        s_y0 = sem("rstd_guess")
        s_gt = sem("gt_ready")
        s_r3f = sem("rows3_full")
        s_r3d = sem("rows3_done")
        s_r3s = [sem(f"rows3_stored{c}") for c in range(NG)]
        s_x02 = [sem(f"x0_x2_broadcast{c}") for c in range(NG)]
        s_x1s = sem("x1_stored")
        s_x1l = sem("x1_by_tile")
        s_x1f = sem("x1_full")
        s_nm = sem("negmax_ready")
        s_e = sem("e_ready")
        s_eu = sem("e_used")
        s_f = sem("feats_ready")
        s_sg = sem("gate_exp")
        s_gate = sem("gate_ready")
        s_gbf = sem("gate_bcast_full")
        s_gx = sem("gate_times_g")
        s_r1 = sem("r1_ready")
        s_norm = sem("group_norm_ready")
        s_g2 = sem("g2_ready")
        s_rt = sem("residual_ready")
        s_xcf = sem("xc_full")
        s_raw = sem("raw_done")
        s_cvf = sem("conv_full")
        s_cvd = sem("conv_done")
        s_zf = sem("z_full")
        s_zd = sem("z_done")
        s_silu = sem("xc_silu_done")
        s_zsilu = sem("z_silu_done")
        s_xdf = sem("xd_full")
        s_xdd = sem("xd_done")
        s_rows = sem("bc_rows_stored")
        s_dtf = sem("dt_full")
        s_dtm = sem("dt_evacuated")
        s_de = sem("dt_exp")
        s_dl = sem("dt_log")
        s_corr = sem("dt_corrected")
        s_dt = sem("dt_ready")
        s_u = sem("u_ready")
        s_dtz = sem("dt_first_steps")
        s_bc = [sem(f"bc_loaded{i}") for i in range(4)]
        s_da = sem("decay_ready")
        s_db = sem("drive_ready")
        s_h = sem("h_ready")
        s_pr = sem("prod_ready")
        s_sum = sem("sum_done")
        s_gy = sem("y_gated")
        s_yg = sem("yg_ready")
        s_of = sem("out_full")
        s_sq = sem("square_done")
        s_on = sem("out_normed")
        s_od = sem("out_done")
        s_st = sem("stored")
        s_bn = sem("bn_stats_done")
        s_dch = sem("dve_chain")

        def bc_there(eng, n, s):
            eng.wait_ge(s_bc[s % 4], n * (16 * NS // 4) + (16 * (s // 4) + 16))

        def seq(t4):
            return t4.rearrange("p (j t) -> p j t", t=T)

        block = ctx.enter_context(nc.Block())

        @block.sync
        def _(sp):
            def rows(n, q):
                sp.wait_ge(s_xdd, n + 1)
                sp.dma_start(bc_rows[q], xd[0:2 * NS, :]).then_inc(s_rows, 16)

            def bcast(n, q, s, fresh):
                if s == 0:
                    sp.wait_ge(s_rows, n * 16 + 16)
                if not fresh:
                    sp.wait_ge(s_pr, n * UNITS + (4 * s - 12 + PROD_CREDIT))
                sp.dma_start(bc[:, s % 4, :, :].rearrange("p i n -> p (i n)"),
                             bc_rows[q, 2 * s:2 * s + 2, :].rearrange("(o i) n -> o (i n)", o=1).to_broadcast([P, 2 * GT])
                             ).then_inc(s_bc[s % 4], 16)

            def step(n, q, g, proj):
                for s in range(NS):
                    if s + 2 < NS:
                        bcast(n, q, s + 2, g == 0 and s < 2)
                    elif proj:
                        if s + 2 == NS:
                            rows(n + 1, 1 - q)
                        bcast(n + 1, 1 - q, s + 2 - NS, False)

            def store(ob, n, j0):
                sp.wait_ge(s_od, n * GTILES + (GTILES + OUT_CREDIT))
                for jj in range(2):
                    sp.dma_start(ob[:, strided(j0, jj), :], osb[64 * jj:64 * jj + 64, :, :]).then_inc(s_st, 16)

            def strided(j0, jj):
                if isinstance(j0, int):
                    return slice(j0 + jj, j0 + GJ, 2)
                return bass.ds(j0 + jj, GTILES, 2)

            for dst, src in ((ident[:], ident_d), (gavg[:], gavg_d),
                             (w3[:], w123.rearrange("(c p) i -> p c i", p=P)),
                             (b3[0:3, :], b123),
                             (win[:], win_t.rearrange("(c p) n -> p c n", p=P)),
                             (cw[:], conv_w.rearrange("(k p) i -> p k i", p=P)),
                             (cb[:], conv_b),
                             (wx[:], wxp.rearrange("(k p) n -> p k n", p=P)),
                             (bdt[:], b_dt),
                             (alog[:], a_log.rearrange("(k p) s -> p k s", p=P)),
                             (dsk[:], d_skip),
                             (wout[:], wout_t.rearrange("(k p) n -> p k n", p=P)),
                             (lnw[:], ln_w.to_broadcast([P, C]))):
                sp.dma_start(dst, src).then_inc(s_w, 16)
            sp.wait_ge(s_pad, 1)
            sp.dma_start(wdt[32:32 + R, :], wdt_t).then_inc(s_w, 16)
            def of_batch(tensor, b):
                part = tensor[b:b + 1] if isinstance(b, int) else tensor[bass.ds(b, 1)]
                return part.rearrange("o t j c -> (o t) j c")

            def load_x(b, chunks):
                for c in chunks:
                    for jj in range(2):
                        sp.dma_start(xin[64 * jj:64 * jj + 64, c, :, :],
                                     of_batch(x, b)[:, GJ * c + jj:GJ * (c + 1):2, :]).then_inc(s_xl[c], 16)

            def softmax_rows(b):
                for c in range(NG + 1):
                    if c < NG:
                        sp.wait_ge(s_r3d, b * NG + (c + 1))
                        sp.dma_start(x02_rows[c], rows3[0:2, c * GT:(c + 1) * GT]).then_inc(s_r3s[c], 16)
                    else:
                        sp.dma_start(x1_row, rows3[2:3, :]).then_inc(s_x1s, 16)
                    if c >= 1:
                        sp.wait_ge(s_r3s[c - 1], b * 16 + 16)
                        sp.dma_start(x02[:, :, (c - 1) * GT:c * GT],
                                     x02_rows[c - 1].rearrange("(o i) n -> o i n", o=1).to_broadcast([P, 2, GT])
                                     ).then_inc(s_x02[c - 1], 16)
                sp.wait_ge(s_x1s, b * 16 + 16)
                sp.dma_start(x1t[0:TILES, :], x1_row.rearrange("o (m p) -> (o m) p", p=P)).then_inc(s_x1l, 16)

            def batch(b, last):
                n0 = b * NG
                ob = of_batch(out, b)
                softmax_rows(b)
                rows(n0, 0)
                bcast(n0, 0, 0, True)
                bcast(n0, 0, 1, True)
                step(n0, 0, 0, True)
                with sp.Fori(0, NG // 2 - 1) as p:
                    n = n0 + 2 * p
                    j0 = 2 * GJ * p
                    step(n + 1, 1, None, True)
                    store(ob, n, j0)
                    step(n + 2, 0, None, True)
                    store(ob, n + 1, j0 + GJ)
                step(n0 + (NG - 1), 1, NG - 1, False)
                if not last:
                    sp.wait_ge(s_h, (n0 + (NG - 1)) * UNITS + H_CREDIT)
                    load_x(b + 1, X_ORDER[:4])
                store(ob, n0 + (NG - 2), GJ * (NG - 2))
                if not last:
                    sp.wait_ge(s_h, (n0 + NG) * UNITS + H_CREDIT)
                    load_x(b + 1, X_ORDER[4:])
                store(ob, n0 + (NG - 1), GJ * (NG - 1))

            load_x(0, X_ORDER)
            if NB > 1:
                with sp.Fori(0, NB - 1) as b:
                    batch(b, False)
            batch(NB - 1, True)
            sp.wait_ge(s_st, STORE_CREDIT + NB * NG * 32)

        @block.tensor
        def _(pe):
            def layer0(b):
                for q, (c, h) in enumerate((c, h) for c in X_ORDER for h in range(CC)):
                    if h == 0:
                        pe.wait_ge(s_xl[c], b * 32 + 32)
                    if q >= 4:
                        pe.wait_ge(s_xtd, b * (NG * CC) + (q - 3))
                    for m in range(GTILES):
                        last = nc.tensor.transpose(psum[:, q % 4, m * P:(m + 1) * P],
                                                   xin[:, c, m, h * P:(h + 1) * P], ident[:])
                        if m == GTILES - 1:
                            last.then_inc(s_xtf, 1)
                pe.wait_ge(s_od, b * (NG * GTILES) + OUT_CREDIT)
                group_stats(b, 0)
                for c in range(NG):
                    for h in range(CC):
                        pe.wait_ge(s_gt, b * (NG * CC) + (CC * c + h + 1))
                    if c >= 4:
                        pe.wait_ge(s_r3d, b * NG + (c - 3))
                    for h in range(CC):
                        last = nc.tensor.matmul(psum[0:3, c % 4, :], w3[:, h, :], gT[:, h, c * GT:(c + 1) * GT],
                                                start=(h == 0), stop=(h == CC - 1))
                    last.then_inc(s_r3f, 1)
                pe.wait_ge(s_x1l, b * 16 + 16)
                nc.tensor.matmul(abank[:, 0:TILES], x1t[0:TILES, :], ident[0:TILES, 0:TILES], start=True,
                                 stop=True).then_inc(s_x1f, 1)
                pe.wait_ge(s_gate, b + 1)
                for c in range(NG):
                    if c >= 4:
                        pe.wait_ge(s_gx, b * (NG * CC) + CC * (c - 3))
                    for m in range(GTILES):
                        i = GTILES * c + m
                        last = nc.tensor.matmul(psum[:, c % 4, m * P:(m + 1) * P],
                                                gt4[:, 4, i:i + 1].to_broadcast([P, P]), ident[:],
                                                start=True, stop=True)
                    last.then_inc(s_gbf, 1)
                group_stats(b, 1)

            def group_stats(b, layer):
                pe.wait_ge(s_mv, 2 * b + (layer + 1))
                nc.tensor.matmul(abank[:, 0:4], gavg[:], mv[:, :, :].rearrange("p c i -> p (c i)"),
                                 start=True, stop=True).then_inc(s_gm, 1)
                pe.wait_ge(s_dev, 2 * b + (layer + 1))
                nc.tensor.matmul(abank[:, 8:10], gavg[:], dev[:], start=True, stop=True).then_inc(s_gd, 1)

            def project(v, n, q, g, prologue):
                i, h = part(XC_PE, v, CC)
                if i is not None:
                    if i == 0 and h == 0:
                        pe.wait_ge(s_g2, n * CC + CC)
                        if g != 0:
                            pe.wait_ge(s_dtm, n * DK)
                            pe.wait_ge(s_zd, n * DK)
                        if g not in (0, 1, 2):
                            pe.wait_ge(s_od, (n - 2) * GTILES + OUT_CREDIT)
                    if i >= 2 and h == 0:
                        pe.wait_ge(s_cvd, n * DK + (i - 1))
                    mm = nc.tensor.matmul(pbank[:, i % 2, :], win[:, h, i * P:(i + 1) * P], g2[:, h, :],
                                          start=(h == 0), stop=(h == CC - 1))
                    if h == CC - 1:
                        mm.then_inc(s_xcf, 1)
                i, tap = part(CONV_PE, v, TAPS)
                if i is not None:
                    if tap == 0:
                        pe.wait_ge(s_raw, n * DK + (i + 1))
                    mm = nc.tensor.matmul(seq(pbank[:, i % 2, :]), cdiag[:, i, tap, :],
                                          raw[:, i % 2, :, tap:tap + T], start=(tap == 0),
                                          stop=(tap == TAPS - 1))
                    if tap == TAPS - 1:
                        mm.then_inc(s_cvf, 1)
                i, h = part(Z_PE, v, CC)
                if i is not None and not prologue:
                    if h == 0 and i < 2:
                        pe.wait_ge(s_cvd, n * DK + (3 + i))
                    elif h == 0:
                        pe.wait_ge(s_zd, n * DK + i)
                    mm = nc.tensor.matmul(pbank[:, min(i, 1), :], win[:, h, DI + i * P:DI + (i + 1) * P],
                                          g2[:, h, :], start=(h == 0), stop=(h == CC - 1))
                    if h == CC - 1:
                        mm.then_inc(s_zf, 1)
                if XD_PE <= v < XD_PE + DK:
                    k = v - XD_PE
                    if prologue:
                        pe.wait_ge(s_cvd, n * DK + max(k + 1, 3))
                    elif k == 0:
                        pe.wait_ge(s_zd, n * DK + 1)
                        pe.wait_ge(s_silu, n + 1)
                    mm = nc.tensor.matmul(pbank[:, 0, :], wx[:, k, :], xc_sb[:, q, k, :],
                                          start=(k == 0), stop=(k == DK - 1))
                    if k == DK - 1:
                        mm.then_inc(s_xdf, 1)
                for i in steps(DT_PE, v):
                    if prologue:
                        for h in range(CC):
                            mm = nc.tensor.matmul(ybank[:, i, :], win[:, h, DI + i * P:DI + (i + 1) * P],
                                                  g2[:, h, :], start=(h == 0), stop=(h == CC - 1))
                        mm.then_inc(s_zf, 1)
                    if i == 0:
                        pe.wait_ge(s_xdd, n + 1)
                    else:
                        pe.wait_ge(s_dtm, n * DK + i)
                    nc.tensor.matmul(pbank[:, 0, :], wdt[:, i * P:(i + 1) * P], xd, start=True,
                                     stop=True).then_inc(s_dtf, 1)

            def output(v, n, proj):
                i, third = part(OUT_PE, v, 3)
                if i is None:
                    return
                bank = pbank[:, OUT_BANK[i], :]
                if third == 0:
                    if i == 0:
                        pe.wait_ge(s_yg, n * DK + DK)
                        pe.wait_ge(s_rt, n * CC + CC)
                    if i == 0 and proj:
                        pe.wait_ge(s_zd, (n + 2) * DK + DK)
                    elif i == 2 and proj:
                        pe.wait_ge(s_dtm, (n + 2) * DK + DK)
                    elif i in (1, 3):
                        pe.wait_ge(s_od, n * GTILES + ((1, 2)[i // 2] + OUT_CREDIT))
                if third < 2:
                    for k in (2 * third, 2 * third + 1):
                        nc.tensor.matmul(bank[:, 0:C], yg[:, k, i * P:(i + 1) * P], wout[:, k, :],
                                         start=(k == 0), stop=(k == DK - 1))
                else:
                    for h in range(CC):
                        last = nc.tensor.transpose(bank[:, C + h * P:C + (h + 1) * P],
                                                   rt[:, h, i * P:(i + 1) * P], ident[:])
                    last.then_inc(s_of, 1)

            def output_last(n):
                pe.wait_ge(s_od, n * GTILES + OUT_CREDIT)
                pe.wait_ge(s_rt, n * CC + CC)
                for k in range(DK):
                    pe.wait_ge(s_yg, n * DK + (k + 1))
                    for i in range(GTILES):
                        nc.tensor.matmul(psum[:, 4 + i, 0:C], yg[:, k, i * P:(i + 1) * P], wout[:, k, :],
                                         start=(k == 0), stop=(k == DK - 1))
                        if k == DK - 1:
                            for h in range(CC):
                                last = nc.tensor.transpose(psum[:, 4 + i, C + h * P:C + (h + 1) * P],
                                                           rt[:, h, i * P:(i + 1) * P], ident[:])
                            last.then_inc(s_of, 1)

            def step(n, q, g, proj, outp):
                for v in range(UNITS):
                    s, k = divmod(v, DK)
                    pe.wait_ge(s_pr, n * UNITS + (v + 1 + PROD_CREDIT))
                    if s == 0 and g != 0:
                        pe.wait_ge(s_gy, n * DK + (k + 1 - DK))
                    elif s == 0:
                        pe.wait_ge(s_zd, n * DK + (k + 1))
                    nc.tensor.matmul(ybank[:, k, :], ident[:], prod[:, v % PRODS, :], start=(s == 0),
                                     stop=(s == NS - 1)).then_inc(s_sum, 1)
                    if proj:
                        project(v, n + 1, 1 - q, -1 if g is None else g + 1, False)
                    if outp:
                        output(v, n - 1, proj)

            pe.wait_ge(s_w, 16 * 14)
            pe.wait_ge(s_wready, 1)
            with pe.Fori(0, NB) as b:
                n0 = b * NG
                layer0(b)
                for v in range(UNITS):
                    project(v, n0, 0, 0, True)
                step(n0, 0, 0, True, False)
                with pe.Fori(0, NG // 2 - 1) as p:
                    n = n0 + 2 * p
                    step(n + 1, 1, None, True, True)
                    step(n + 2, 0, None, True, True)
                step(n0 + (NG - 1), 1, NG - 1, False, True)
                output_last(n0 + (NG - 1))

        @block.scalar
        def _(act):
            def exp_ln_table():
                nc.scalar.preload_act_table_set("natural_log_exp_and_others")

            def group_stats(b, layer):
                act.wait_ge(s_var, 2 * b + (layer + 1))
                nc.scalar.activation(lnv[:], gvar[:], ACT.Ln).then_inc(s_ln, 1)
                act.wait_ge(s_ln, 2 * b + (layer + 1))
                nc.scalar.activation(y0[:], lnv[:], ACT.Exp, scale=-0.5).then_inc(s_y0, 1)

            def layer0(b):
                for q, (c, h) in enumerate((c, h) for c in X_ORDER for h in range(CC)):
                    act.wait_ge(s_xtf, b * (NG * CC) + (q + 1))
                    nc.scalar.activation(xT[:, h, c * GT:(c + 1) * GT], psum[:, q % 4, :],
                                         ACT.Copy).then_inc(s_xtd, 1)
                group_stats(b, 0)
                for c in range(NG):
                    act.wait_ge(s_r3f, b * NG + (c + 1))
                    nc.scalar.activation(rows3[:, c * GT:(c + 1) * GT], psum[0:3, c % 4, :], ACT.Identity,
                                         bias=b3[0:3, 0:1]).then_inc(s_r3d, 1)
                act.wait_ge(s_nm, b + 1)
                for i in range(TILES):
                    if i >= 2:
                        act.wait_ge(s_eu, b * TILES + (i - 1))
                    nc.scalar.activation(ee[:, i % 2, :], x0b, ACT.Exp, bias=nm[:, 2, i:i + 1],
                                         scale=x1c[:, i:i + 1], accum_out=den[:, i:i + 1]).then_inc(s_e, 1)
                act.wait_ge(s_f, b + 1)
                nc.scalar.activation(gt4[:, 2, :], gt4[:, 1, :], ACT.Exp, scale=-1.0).then_inc(s_sg, 1)
                group_stats(b, 1)

            def project(v, n, q, first, prologue):
                for i in steps(CONV_ACT, v):
                    act.wait_ge(s_cvf, n * DK + (i + 1))
                    if i == 0 and not first:
                        act.wait_ge(s_gy, (n - 1) * DK)
                    nc.scalar.activation(xc_sb[:, q, i, :], pbank[:, i % 2, :], ACT.Silu if prologue else ACT.Identity,
                                         bias=cb[:, i:i + 1]).then_inc(s_cvd, 1)
                for i in steps(XC_ACT, v):
                    act.wait_ge(s_xcf, n * DK + (i + 1))
                    if i >= 2:
                        act.wait_ge(s_cvf, n * DK + (i - 1))
                    nc.scalar.activation(raw[:, i % 2, :, TAPS - 1:], seq(pbank[:, i % 2, :]),
                                         ACT.Copy).then_inc(s_raw, 1)
                for i in () if prologue else steps(Z_ACT, v):
                    act.wait_ge(s_zf, n * DK + (i + 1))
                    if i == 0 and not first:
                        act.wait_ge(s_yg, (n - 1) * DK)
                    nc.scalar.activation(zs_sb[:, q, i, :], pbank[:, min(i, 1), :], ACT.Copy).then_inc(s_zd, 1)
                if v == XD_ACT:
                    act.wait_ge(s_xdf, n + 1)
                    nc.scalar.activation(xd, pbank[:, 0, :], ACT.Copy).then_inc(s_xdd, 1)
                for i in steps(DT_ACT, v):
                    act.wait_ge(s_dtf, n * DK + (i + 1))
                    if not (prologue and i < 2):
                        act.wait_ge(s_corr, n * (3 * DK) + 3 * (i - 1))
                    nc.scalar.activation(te[:, i % 2, :], pbank[:, 0, :], ACT.Abs, bias=bdt[:, i:i + 1])
                    nc.scalar.activation(dt_sb[:, q, i, :], pbank[:, 0, :], ACT.Relu,
                                         bias=bdt[:, i:i + 1]).then_inc(s_dtm, 1)
                for i in steps(DT_ACT, v - 1):
                    act.wait_ge(s_dtm, n * DK + (i + 1))
                    nc.scalar.activation(te[:, i % 2, :], te[:, i % 2, :], ACT.Exp, scale=-1.0).then_inc(s_de, 1)
                for i in steps(DT_ACT, v - 2):
                    act.wait_ge(s_de, n * DK + (i + 1))
                    nc.scalar.activation(tl[:, i % 2, :], te[:, i % 2, :], ACT.Ln, bias=1.0).then_inc(s_dl, 1)

            def span(g):
                return slice(g * GT, (g + 1) * GT) if isinstance(g, int) else bass.ds(g * GT, GT)

            def normalise(h, n, g):
                nc.scalar.activation(g2[:, h, :], xT[:, h, span(g)], ACT.Identity, scale=gn[:, 0, h:h + 1],
                                     bias=gn[:, 1, h:h + 1]).then_inc(s_g2, 1)

            def residual(h, n, g):
                nc.scalar.activation(rt[:, h, :], xT[:, h, span(g)], ACT.Identity, scale=rp1[:, h:h + 1],
                                     bias=gn[:, 1, h:h + 1]).then_inc(s_rt, 1)

            def silu(n_xc, q_xc, n_z, q_z):
                if n_xc is not None:
                    act.wait_ge(s_cvd, n_xc * DK + DK)
                    nc.scalar.activation(xc_sb[:, q_xc, :, :], xc_sb[:, q_xc, :, :], ACT.Silu).then_inc(s_silu, 1)
                act.wait_ge(s_zd, n_z * DK + DK)
                nc.scalar.activation(zs_sb[:, q_z, :, :], zs_sb[:, q_z, :, :], ACT.Silu).then_inc(s_zsilu, 1)
                exp_ln_table()

            def square(i, n, bank):
                act.wait_ge(s_of, n * GTILES + (i + 1))
                nc.scalar.activation(sqj[:], bank[:, 0:C], ACT.Square, accum_out=ssq[:, i:i + 1]).then_inc(s_sq, 1)

            def log_mean(i, n):
                act.wait_ge(s_sq, n * (3 * GTILES) + (3 * i + 1))
                nc.scalar.activation(lms[:, i:i + 1], ssq[:, i:i + 1], ACT.Ln, scale=1.0 / C,
                                     bias=eps[:, 0:1]).then_inc(s_sq, 1)

            def inv_root(i, n):
                act.wait_ge(s_sq, n * (3 * GTILES) + (3 * i + 2))
                nc.scalar.activation(rms[:, i:i + 1], lms[:, i:i + 1], ACT.Exp, scale=-0.5).then_inc(s_sq, 1)

            def output(v, n):
                for i in range(GTILES):
                    if v == OUT_SQUARE[i]:
                        square(i, n, pbank[:, OUT_BANK[i], :])
                    if v == OUT_LN[i]:
                        log_mean(i, n)
                    if v == OUT_EXP[i]:
                        inv_root(i, n)

            def step(n, q, g, first, proj, outp):
                for v in range(UNITS):
                    s, k = divmod(v, DK)
                    if s == 0:
                        act.wait_ge(s_dtz, n * DK + (k + 1))
                    act.wait_ge(s_pr, n * UNITS + (v - 1 + PROD_CREDIT))
                    nc.scalar.activation(hbank[:, v % 2, :], dt_sb[:, q, k, :], ACT.Exp,
                                         scale=amat[:, k, s:s + 1]).then_inc(s_da, 1)
                    if proj:
                        for h in steps(NORM_ACT, v):
                            act.wait_ge(s_zf, n * DK + DK)
                            normalise(h, n + 1, g + 1)
                        project(v, n + 1, 1 - q, first, False)
                    if v == SILU_ACT:
                        silu(n + 1 if proj else None, 1 - q, n, q)
                    if outp:
                        for h in steps(RT_ACT, v):
                            residual(h, n - 1, g - 1)
                        output(v, n - 1)

            act.wait_ge(s_w, 16 * 14)
            nc.scalar.activation(amat[:], alog[:], ACT.Exp).then_inc(s_aexp, 1)
            act.wait_ge(s_wready, 1)
            with act.Fori(0, NB) as b:
                n0 = b * NG
                exp_ln_table()
                layer0(b)
                act.wait_ge(s_norm, b + 1)
                for h in range(CC):
                    normalise(h, n0, 0)
                for v in range(UNITS):
                    project(v, n0, 0, True, True)
                    if v == SILU_ACT:
                        act.wait_ge(s_cvd, n0 * DK + DK)
                        nc.scalar.activation(lnv[:], lnv[:], ACT.Copy).then_inc(s_silu, 1)
                        exp_ln_table()
                for i in range(DK):
                    act.wait_ge(s_zf, n0 * DK + (i + 1))
                    nc.scalar.activation(zs_sb[:, 0, i, :], ybank[:, i, :], ACT.Copy).then_inc(s_zd, 1)
                step(n0, 0, 0, True, True, False)
                with act.Fori(0, NG // 2 - 1) as p:
                    n = n0 + 2 * p
                    exp_ln_table()
                    step(n + 1, 1, 2 * p + 1, False, True, True)
                    step(n + 2, 0, 2 * p + 2, False, True, True)
                exp_ln_table()
                step(n0 + (NG - 1), 1, NG - 1, False, False, True)
                for h in range(CC):
                    residual(h, n0 + (NG - 1), NG - 1)
                for i in range(GTILES):
                    square(i, n0 + (NG - 1), psum[:, 4 + i, :])
                    log_mean(i, n0 + (NG - 1))
                    inv_root(i, n0 + (NG - 1))
                act.wait_ge(s_of, (b + 1) * (NG * GTILES))

        @block.gpsimd
        def _(pool):
            def project(v, n, q, prologue):
                for i in () if prologue else steps(DT_POOL, v):
                    pool.wait_ge(s_corr, n * (3 * DK) + (3 * i + 3))
                    nc.gpsimd.tensor_tensor(dt_sb[:, q, i, :], dt_sb[:, q, i, :], tc[:, i % 2, :],
                                            ALU.add).then_inc(s_dt, 1)
                for i in steps(U_POOL, v):
                    pool.wait_ge(s_dt, n * DK + (i + 1))
                    nc.gpsimd.tensor_tensor(u_sb[:, q, i, :], dt_sb[:, q, i, :], xc_sb[:, q, i, :],
                                            ALU.mult).then_inc(s_u, 1)
                    pool.wait_ge(s_u, n * DK + (i + 1))
                    nc.gpsimd.tensor_tensor(seq(dt_sb[:, q, i, :])[:, :, 0:1], half_big[:], half_big[:],
                                            ALU.add).then_inc(s_dtz, 1)

            def gate(n, q, k):
                pool.wait_ge(s_zsilu, n + 1)
                pool.wait_ge(s_gy, n * DK + (k + 1))
                nc.gpsimd.tensor_tensor(yg[:, k, :], yg[:, k, :], zs_sb[:, q, k, :], ALU.mult).then_inc(s_yg, 1)

            def step(n, q, proj, gate_prev):
                for v in range(0, UNITS, 2):
                    s, k = divmod(v, DK)
                    if s == 0:
                        pool.wait_ge(s_u, n * DK + (k + 2))
                    bc_there(pool, n, s)
                    pool.wait_ge(s_h, n * UNITS + (v - 2 + H_CREDIT))
                    nc.gpsimd.tensor_tensor(drive[:, (v // 2) % 2, :, :], u_sb[:, q, k:k + 2, :],
                                            bc[:, s % 4, 0:1, :].to_broadcast([P, 2, GT]),
                                            ALU.mult).then_inc(s_db, 1)
                    if gate_prev:
                        for kg in steps(GATE_POOL, v):
                            gate(n - 1, 1 - q, kg)
                    if proj:
                        for w in (v, v + 1):
                            project(w, n + 1, 1 - q, False)

            with pool.Fori(0, NB) as b:
                n0 = b * NG
                for c in range(NG):
                    for h in range(CC):
                        pool.wait_ge(s_gx, b * (NG * CC) + (CC * c + h + 1))
                        nc.gpsimd.tensor_tensor(xT[:, h, c * GT:(c + 1) * GT], xT[:, h, c * GT:(c + 1) * GT],
                                                gT[:, h, c * GT:(c + 1) * GT], ALU.add).then_inc(s_r1, 1)
                for v in range(UNITS):
                    project(v, n0, 0, True)
                step(n0, 0, True, False)
                with pool.Fori(0, NG // 2 - 1) as p:
                    n = n0 + 2 * p
                    step(n + 1, 1, True, True)
                    step(n + 2, 0, True, True)
                step(n0 + (NG - 1), 1, False, True)
                for k in range(DK):
                    gate(n0 + (NG - 1), 1, k)

        @block.vector
        def _(dve):
            def group_stats(b, layer):
                dve.wait_ge(s_bn, b * (2 * NG * CC) + (layer + 1) * NG * CC)
                nc.vector.tensor_copy(spare[:, 7:8], stats[:, 0, 0, 0:1])
                for h in range(CC):
                    last = nc.vector.bn_aggr(mv[:, h, :], stats[:, h, :, :].rearrange("p c i -> p (c i)"))
                last.then_inc(s_mv, 1)
                dve.wait_ge(s_gm, 2 * b + (layer + 1))
                link(b, nc.vector.tensor_copy(gs[:], abank[:, 0:4]))
                gsv = gs[:].rearrange("p (c i) -> p c i", c=CC)
                link(b, nc.vector.tensor_tensor(nt[:, 0, :], mv[:, :, 0], gsv[:, :, 0], ALU.subtract))
                nc.vector.tensor_tensor(dev[:], nt[:, 0, :], nt[:, 0, :], ALU.mult).then_inc(s_dev, 1)
                dve.wait_ge(s_gd, 2 * b + (layer + 1))
                nc.vector.scalar_tensor_tensor(out=gvar[:], in0=abank[:, 8:10], scalar=1e-5, in1=gsv[:, :, 1],
                                               op0=ALU.add, op1=ALU.add).then_inc(s_var, 1)
                dve.wait_ge(s_y0, 2 * b + (layer + 1))
                link(b, nc.vector.tensor_tensor(nt[:, 0, :], y0[:], y0[:], ALU.mult))
                link(b, nc.vector.tensor_tensor(nt[:, 1, :], nt[:, 0, :], gvar[:], ALU.mult))
                link(b, nc.vector.tensor_scalar(nt[:, 0, :], nt[:, 1, :], -0.5, 1.5, ALU.mult, ALU.add))
                link(b, nc.vector.tensor_tensor(gn[:, 0, :], y0[:], nt[:, 0, :], ALU.mult))
                link(b, nc.vector.scalar_tensor_tensor(out=gn[:, 1, :], in0=gsv[:, :, 0], scalar=-1.0,
                                                       in1=gn[:, 0, :], op0=ALU.mult, op1=ALU.mult))

            count = [0]

            def link(b, ins):
                count[0] += 1
                ins.then_inc(s_dch, 1)
                dve.wait_ge(s_dch, b * DVE_LINKS + count[0])

            def layer0(b):
                for q, (c, h) in enumerate((c, h) for c in X_ORDER for h in range(CC)):
                    dve.wait_ge(s_xtd, b * (NG * CC) + (q + 1))
                    nc.vector.bn_stats(stats[:, h, c, :], xT[:, h, c * GT:(c + 1) * GT]).then_inc(s_bn, 1)
                group_stats(b, 0)
                for c in range(NG):
                    for h in range(CC):
                        nc.vector.tensor_scalar(gT[:, h, c * GT:(c + 1) * GT], xT[:, h, c * GT:(c + 1) * GT],
                                                gn[:, 0, h:h + 1], gn[:, 1, h:h + 1], ALU.mult,
                                                ALU.add).then_inc(s_gt, 1)
                for c in range(NG):
                    dve.wait_ge(s_x02[c], b * 16 + 16)
                    nc.vector.tensor_reduce(mxs[:, 0, c:c + 1], x0b[:, c * GT:(c + 1) * GT], AX.X, ALU.max)
                    last = nc.vector.tensor_reduce(mxs[:, 1, c:c + 1], x0b[:, c * GT:(c + 1) * GT], AX.X, ALU.min)
                link(b, last)
                nc.vector.tensor_reduce(mm[:, 0:1], mxs[:, 0, :], AX.X, ALU.max)
                link(b, nc.vector.tensor_reduce(mm[:, 1:2], mxs[:, 1, :], AX.X, ALU.min))
                dve.wait_ge(s_x1f, b + 1)
                link(b, nc.vector.tensor_copy(x1c[:], abank[:, 0:TILES]))
                nc.vector.tensor_scalar(nm[:, 0, :], x1c[:], mm[:, 0:1], None, ALU.mult)
                link(b, nc.vector.tensor_scalar(nm[:, 1, :], x1c[:], mm[:, 1:2], None, ALU.mult))
                link(b, nc.vector.tensor_tensor(nm[:, 0, :], nm[:, 0, :], nm[:, 1, :], ALU.max))
                nc.vector.tensor_scalar(nm[:, 2, :], nm[:, 0, :], -1.0, None, ALU.mult).then_inc(s_nm, 1)
                for i in range(TILES):
                    dve.wait_ge(s_e, b * TILES + (i + 1))
                    nc.vector.tensor_tensor_reduce(out=ee[:, i % 2, :], in0=ee[:, i % 2, :], in1=x2b, scale=1.0,
                                                   scalar=0.0, op0=ALU.mult, op1=ALU.add,
                                                   accum_out=num[:, i:i + 1]).then_inc(s_eu, 1)
                dve.wait_ge(s_eu, b * TILES + TILES)
                link(b, nc.vector.reciprocal(gt4[:, 0, :], den[:]))
                nc.vector.tensor_tensor(gt4[:, 1, :], num[:], gt4[:, 0, :], ALU.mult).then_inc(s_f, 1)
                dve.wait_ge(s_sg, b + 1)
                link(b, nc.vector.tensor_scalar(gt4[:, 3, :], gt4[:, 2, :], 1.0, None, ALU.add))
                nc.vector.reciprocal(gt4[:, 4, :], gt4[:, 3, :]).then_inc(s_gate, 1)
                for c in range(NG):
                    dve.wait_ge(s_gbf, b * NG + (c + 1))
                    for h in range(CC):
                        nc.vector.tensor_tensor(gT[:, h, c * GT:(c + 1) * GT], gT[:, h, c * GT:(c + 1) * GT],
                                                psum[:, c % 4, :], ALU.mult).then_inc(s_gx, 1)
                    if c:
                        r1_stats(b, c - 1)
                r1_stats(b, NG - 1)
                group_stats(b, 1)
                nc.vector.tensor_scalar(rp1[:], gn[:, 0, :], 1.0, None, ALU.add).then_inc(s_norm, 1)

            def r1_stats(b, c):
                for h in range(CC):
                    dve.wait_ge(s_r1, b * (NG * CC) + (CC * c + h + 1))
                    nc.vector.bn_stats(stats[:, h, c, :], xT[:, h, c * GT:(c + 1) * GT]).then_inc(s_bn, 1)

            def project(v, n, prologue):
                i, third = part(DT_DVE, v, 3)
                if third == 0:
                    if not (prologue and i < 2):
                        dve.wait_ge(s_dt, n * DK + (i - 1))
                    dve.wait_ge(s_de, n * DK + (i + 1))
                    nc.vector.tensor_scalar(tc[:, i % 2, :], te[:, i % 2, :], 1.0, 1.0, ALU.add, ALU.subtract).then_inc(s_corr, 1)
                elif third == 1:
                    dve.wait_ge(s_corr, n * (3 * DK) + (3 * i + 1))
                    nc.vector.tensor_tensor(tc[:, i % 2, :], te[:, i % 2, :], tc[:, i % 2, :], ALU.subtract).then_inc(s_corr, 1)
                elif third == 2:
                    dve.wait_ge(s_dl, n * DK + (i + 1))
                    dve.wait_ge(s_corr, n * (3 * DK) + (3 * i + 2))
                    nc.vector.tensor_tensor(tc[:, i % 2, :], tl[:, i % 2, :], tc[:, i % 2, :], ALU.add).then_inc(s_corr, 1)
                    if prologue:
                        dve.wait_ge(s_corr, n * (3 * DK) + (3 * i + 3))
                        nc.vector.tensor_tensor(dt_sb[:, 0, i, :], dt_sb[:, 0, i, :], tc[:, i % 2, :],
                                                ALU.add).then_inc(s_dt, 1)

            def scale_output(i, n, bank):
                dve.wait_ge(s_sq, n * (3 * GTILES) + (3 * i + 3))
                if i == 0:
                    dve.wait_ge(s_st, n * 32 + STORE_CREDIT)
                nc.vector.scalar_tensor_tensor(out=osb[:, i, :], in0=bank[:, 0:C], scalar=rms[:, i:i + 1],
                                               in1=lnw[:], op0=ALU.mult, op1=ALU.mult).then_inc(s_on, 1)

            def add_residual(i, n, bank):
                dve.wait_ge(s_on, n * GTILES + (i + 1))
                nc.vector.tensor_tensor(osb[:, i, :], osb[:, i, :], bank[:, C:2 * C],
                                        ALU.add).then_inc(s_od, 1)

            def gate(n, q, k):
                dve.wait_ge(s_sum, n * UNITS + (UNITS - DK + k + 1 + SUM_CREDIT))
                nc.vector.scalar_tensor_tensor(out=yg[:, k, :], in0=xc_sb[:, q, k, :], scalar=dsk[:, k:k + 1],
                                               in1=ybank[:, k, :], op0=ALU.mult, op1=ALU.add).then_inc(s_gy, 1)

            def step(n, q, proj, prev):
                for v in range(UNITS):
                    s, k = divmod(v, DK)
                    dve.wait_ge(s_da, n * UNITS + (v + 1))
                    if v % 2 == 0:
                        dve.wait_ge(s_db, n * (UNITS // 2) + (v // 2 + 1))
                    nc.vector.tensor_tensor_scan(hbank[:, v % 2, :], hbank[:, v % 2, :],
                                                 drive[:, (v // 2) % 2, v % 2, :], 0.0, ALU.mult,
                                                 ALU.add).then_inc(s_h, 1)
                    if prev and v < DK:
                        gate(n - 1, 1 - q, v)
                    if proj:
                        project(v, n + 1, False)
                    if prev:
                        for i in steps(OUT_DVE, v):
                            scale_output(i, n - 1, pbank[:, OUT_BANK[i], :])
                    if k == 0:
                        bc_there(dve, n, s)
                    dve.wait_ge(s_sum, n * UNITS + (v + 1 - PRODS + SUM_CREDIT))
                    dve.wait_ge(s_h, n * UNITS + (v + 1 + H_CREDIT))
                    nc.vector.tensor_tensor(prod[:, v % PRODS, :], hbank[:, v % 2, :], bc[:, s % 4, 1, :],
                                            ALU.mult).then_inc(s_pr, 1)
                    if prev:
                        for i in steps(OUT_DVE, v):
                            add_residual(i, n - 1, pbank[:, OUT_BANK[i], :])

            nc.vector.memset(wdt[:], 0.0).then_inc(s_pad, 1)
            nc.vector.memset(eps[:], 1e-6)
            nc.vector.memset(half_big[:], BIG_DT / 2)
            nc.vector.memset(raw[:], 0.0)
            for i, (credited, credit) in enumerate(((s_h, H_CREDIT), (s_pr, PROD_CREDIT), (s_sum, SUM_CREDIT),
                                                    (s_od, OUT_CREDIT),
                                                    (s_st, STORE_CREDIT))):
                nc.vector.memset(spare[:, i:i + 1], 0.0).then_inc(credited, credit)
            dve.wait_ge(s_w, 16 * 14)
            for k in range(DK):
                for tap in range(TAPS):
                    nc.vector.tensor_scalar(cdiag[:, k, tap, :], ident[:], cw[:, k, tap:tap + 1], None, ALU.mult)
            dve.wait_ge(s_aexp, 1)
            nc.vector.tensor_scalar(amat[:], amat[:], MIN_A, -1.0, ALU.max, ALU.mult).then_inc(s_wready, 1)
            dve.wait_ge(s_wready, 1)
            with dve.Fori(0, NB) as b:
                n0 = b * NG
                layer0(b)
                for v in range(UNITS):
                    project(v, n0, True)
                step(n0, 0, True, False)
                with dve.Fori(0, NG // 2 - 1) as p:
                    n = n0 + 2 * p
                    step(n + 1, 1, True, True)
                    step(n + 2, 0, True, True)
                step(n0 + (NG - 1), 1, False, True)
                for k in range(DK):
                    gate(n0 + (NG - 1), 1, k)
                for i in range(GTILES):
                    scale_output(i, n0 + (NG - 1), psum[:, 4 + i, :])
                    add_residual(i, n0 + (NG - 1), psum[:, 4 + i, :])
                assert count[0] == DVE_LINKS, count


def _arrays(i):
    import numpy as np
    f = lambda a: np.ascontiguousarray(np.asarray(a))
    cols = lambda a: f(np.asarray(a).reshape(DK, P).T)
    wxp = f(i["L1_conv_W_xproj"])
    dt_rows, bc_rows = wxp[:R], wxp[R:]
    lay = np.zeros((DI, P), np.float32)
    lay[:, 0:2 * NS:2] = bc_rows[:NS].T
    lay[:, 1:2 * NS:2] = bc_rows[NS:].T
    lay[:, 2 * NS:2 * NS + R] = dt_rows.T
    return {
        "x": f(i["x"]),
        "w123": f(np.stack([i["L0_conv_w1"], i["L0_conv_w3"], i["L0_conv_w2"]], 1)),
        "b123": f(np.stack([i["L0_conv_b1"], i["L0_conv_b3"], i["L0_conv_b2"]])),
        "win_t": f(np.asarray(i["L1_conv_W_in"]).T),
        "conv_w": f(i["L1_conv_conv_w"]),
        "conv_b": cols(i["L1_conv_conv_b"]),
        "wxp": lay,
        "wdt_t": f(np.asarray(i["L1_conv_W_dt"]).T),
        "b_dt": cols(i["L1_conv_b_dt"]),
        "a_log": f(i["L1_conv_A_log"]),
        "d_skip": cols(i["L1_conv_D_skip"]),
        "wout_t": f(np.asarray(i["L1_conv_W_out"]).T),
        "ln_w": f(i["L1_conv_ln_w"])[None, :],
        "ident_d": np.eye(P, dtype=np.float32),
        "gavg_d": np.kron(np.eye(P // 8), np.full((8, 8), 0.125)).astype(np.float32),
    }


def kernel(**inputs):
    import numpy as np
    import concourse.bacc as bacc
    from concourse.bass_utils import run_bass_kernel_spmd as run

    nc = bacc.Bacc("TRN2", target_bir_lowering=False, num_devices=1)
    arrays = _arrays(inputs)
    aps = [nc.dram_tensor(name, a.shape, mybir.dt.from_np(a.dtype), kind="ExternalInput").ap()
           for name, a in arrays.items()]
    out = nc.dram_tensor("out", arrays["x"].shape, F32, kind="ExternalOutput").ap()
    build(nc, *aps, out)
    return run(nc, [arrays], core_ids=[0]).results[0]["out"]
```
